# Optimizing a Trainium2 kernel written in Bass

```python
import numpy as np
import jax
import jax.numpy as jnp

def _softmax(x, axis=-1):
    return jax.nn.softmax(x, axis=axis)

def _gelu(x):
    return jax.nn.gelu(x, approximate=True)

def _silu(x):
    return jax.nn.silu(x)

def _sigmoid(x):
    return jax.nn.sigmoid(x)

def _layernorm(x, axis=-1, eps=1e-05):
    m = jnp.mean(x, axis=axis, keepdims=True)
    v = jnp.var(x, axis=axis, keepdims=True)
    return (x - m) / jnp.sqrt(v + eps)

def _scatter_add(tgt, idx, src, axis=0):
    return tgt.at[idx].add(src)

def _segment_sum(src, seg, n):
    return jax.ops.segment_sum(src, seg, n)
kernel_name = 'mk_early_fusion_d1_tok_img768_r4_8fd924'

def setup_inputs(seed: int=0):
    np.random.seed(seed)
    _w = jnp.asarray

    def _rec_inputs():
        import jax
        import jax.numpy as jnp
        _rk = jax.random.key(seed)
        x = -0.000356955 + 1 * jax.random.normal(jax.random.fold_in(_rk, 1), (64, 96, 96, 3), jnp.float32)
        txt = 0.000308838 + 0.999433 * jax.random.normal(jax.random.fold_in(_rk, 2), (64, 32, 192), jnp.float32)
        return (x, txt)
    x, txt = _rec_inputs()

    def _L0_tok_setup():
        import jax, jax.numpy as jnp
        import numpy as np
        PATCH = 16
        EMBED = 192
        key = jax.random.key(seed)
        k1, k2 = jax.random.split(key)
        B, H, W_, C = (128, 224, 224, 3)
        images = jax.random.normal(k1, (B, H, W_, C), dtype=jnp.float32)
        patch_dim = PATCH * PATCH * C
        W = jax.random.normal(k2, (patch_dim, EMBED), dtype=jnp.float32) * patch_dim ** (-0.5)
        b = jnp.zeros((EMBED,), dtype=jnp.float32)
        return {'images': images, 'W': W, 'b': b}
    _L0_tok_all = _L0_tok_setup()
    _L0_tok_in = {k: v for k, v in _L0_tok_all.items() if k in ('W', 'b')}
    del _L0_tok_all

    def _L0_attn_setup():
        import jax, jax.numpy as jnp
        import numpy as np
        DIM = 192
        HEADS = 12
        DH = DIM // HEADS
        M = 64
        EPS = 0.0001

        def softmax_kernel(data, proj, is_query):
            data_normalizer = data.shape[-1] ** (-0.25)
            ratio = proj.shape[0] ** (-0.5)
            data_dash = jnp.einsum('bhsd,md->bhsm', data_normalizer * data, proj)
            diag = 0.5 * data_normalizer ** 2 * jnp.sum(data * data, axis=-1, keepdims=True)
            if is_query:
                stab = jnp.max(data_dash, axis=-1, keepdims=True)
            else:
                stab = jnp.max(data_dash, axis=(-2, -1), keepdims=True)
            stab = jax.lax.stop_gradient(stab)
            return ratio * (jnp.exp(data_dash - diag - stab) + EPS)
        key = jax.random.key(seed)
        kx, kq, kk, kv, ko, kp = jax.random.split(key, 6)
        B, S = (8, 1024)
        w_scale = DIM ** (-0.5)
        return {'x': jax.random.normal(kx, (B, S, DIM), jnp.float32), 'Wq': jax.random.normal(kq, (DIM, DIM), jnp.float32) * w_scale, 'Wk': jax.random.normal(kk, (DIM, DIM), jnp.float32) * w_scale, 'Wv': jax.random.normal(kv, (DIM, DIM), jnp.float32) * w_scale, 'Wo': jax.random.normal(ko, (DIM, DIM), jnp.float32) * w_scale, 'proj': jax.random.normal(kp, (M, DH), jnp.float32)}
    _L0_attn_all = _L0_attn_setup()
    _L0_attn_in = {k: v for k, v in _L0_attn_all.items() if k in ('Wq', 'Wk', 'Wv', 'Wo', 'proj')}
    del _L0_attn_all

    def _L0_ffn_setup():
        import jax, jax.numpy as jnp
        import numpy as np
        B, S, D_IN, D_HID, D_OUT = (32, 128, 192, 768, 192)
        key = jax.random.key(seed)
        k1, k2, k3, k4 = jax.random.split(key, 4)
        init_k = float(np.sqrt(1.0 / D_IN))
        init_k2 = float(np.sqrt(1.0 / D_HID))
        x = jax.random.normal(k1, (B, S, D_IN), dtype=jnp.float32)
        in_weight = jax.random.uniform(k2, (D_HID, D_IN), dtype=jnp.float32, minval=-init_k, maxval=init_k)
        in_bias = jax.random.uniform(k3, (D_HID,), dtype=jnp.float32, minval=-init_k, maxval=init_k)
        out_weight = jax.random.uniform(k4, (D_HID, D_OUT), dtype=jnp.float32, minval=-init_k2, maxval=init_k2)
        return {'x': x, 'in_weight': in_weight, 'in_bias': in_bias, 'out_weight': out_weight}
    _L0_ffn_all = _L0_ffn_setup()
    _L0_ffn_in = {k: v for k, v in _L0_ffn_all.items() if k in ('in_weight', 'in_bias', 'out_weight')}
    del _L0_ffn_all
    return {'x': x, 'txt': txt, 'L0_tok_W': _L0_tok_in['W'], 'L0_tok_b': _L0_tok_in['b'], 'L0_attn_Wq': _L0_attn_in['Wq'], 'L0_attn_Wk': _L0_attn_in['Wk'], 'L0_attn_Wv': _L0_attn_in['Wv'], 'L0_attn_Wo': _L0_attn_in['Wo'], 'L0_attn_proj': _L0_attn_in['proj'], 'L0_ffn_in_weight': _L0_ffn_in['in_weight'], 'L0_ffn_in_bias': _L0_ffn_in['in_bias'], 'L0_ffn_out_weight': _L0_ffn_in['out_weight']}

def reference(x, txt, L0_tok_W, L0_tok_b, L0_attn_Wq, L0_attn_Wk, L0_attn_Wv, L0_attn_Wo, L0_attn_proj, L0_ffn_in_weight, L0_ffn_in_bias, L0_ffn_out_weight):
    import jax
    import jax.numpy as jnp

    def _L0_tok_ref(images, W, b):
        import jax, jax.numpy as jnp
        import numpy as np
        PATCH = 16
        EMBED = 192
        B, H, Wd, C = images.shape
        nh, nw = (H // PATCH, Wd // PATCH)
        x = images.reshape(B, nh, PATCH, nw, PATCH, C)
        x = x.transpose(0, 1, 3, 2, 4, 5)
        x = x.reshape(B, nh * nw, PATCH * PATCH * C)
        return jnp.einsum('bnd,de->bne', x, W) + b

    def _L0_attn_ref(x, Wq, Wk, Wv, Wo, proj):
        import jax, jax.numpy as jnp
        import numpy as np
        DIM = 192
        HEADS = 12
        DH = DIM // HEADS
        M = 64
        EPS = 0.0001

        def softmax_kernel(data, proj, is_query):
            data_normalizer = data.shape[-1] ** (-0.25)
            ratio = proj.shape[0] ** (-0.5)
            data_dash = jnp.einsum('bhsd,md->bhsm', data_normalizer * data, proj)
            diag = 0.5 * data_normalizer ** 2 * jnp.sum(data * data, axis=-1, keepdims=True)
            if is_query:
                stab = jnp.max(data_dash, axis=-1, keepdims=True)
            else:
                stab = jnp.max(data_dash, axis=(-2, -1), keepdims=True)
            stab = jax.lax.stop_gradient(stab)
            return ratio * (jnp.exp(data_dash - diag - stab) + EPS)
        B, S, _ = x.shape

        def split_heads(t):
            return t.reshape(B, S, HEADS, DH).transpose(0, 2, 1, 3)
        q = split_heads(x @ Wq)
        k = split_heads(x @ Wk)
        v = split_heads(x @ Wv)
        qp = softmax_kernel(q, proj, is_query=True)
        kp = softmax_kernel(k, proj, is_query=False)
        k_sum = jnp.sum(kp, axis=2)
        d_inv = 1.0 / jnp.einsum('bhsm,bhm->bhs', qp, k_sum)
        ctx = jnp.einsum('bhsm,bhsd->bhmd', kp, v)
        out = jnp.einsum('bhsm,bhmd,bhs->bhsd', qp, ctx, d_inv)
        out = out.transpose(0, 2, 1, 3).reshape(B, S, DIM)
        return out @ Wo

    def _L0_ffn_ref(x, in_weight, in_bias, out_weight):
        import jax, jax.numpy as jnp
        import numpy as np
        B, S, D_IN, D_HID, D_OUT = (32, 128, 192, 768, 192)
        lead = x.shape[:-1]
        xt = x.reshape(-1, in_weight.shape[1])
        h = jax.nn.gelu(jnp.einsum('td,hd->th', xt, in_weight) + in_bias, approximate=False)
        out = jnp.einsum('th,ho->to', h, out_weight)
        return out.reshape(*lead, out_weight.shape[1])
    h = _L0_tok_ref(x, L0_tok_W, L0_tok_b)
    h = jnp.concatenate([h, txt], axis=1)
    h = h + _L0_attn_ref(_layernorm(h, axis=-1), L0_attn_Wq, L0_attn_Wk, L0_attn_Wv, L0_attn_Wo, L0_attn_proj)
    h = h + _L0_ffn_ref(_layernorm(h, axis=-1), L0_ffn_in_weight, L0_ffn_in_bias, L0_ffn_out_weight)
    return h

_drawn_inputs = setup_inputs


def setup_inputs(seed=0):
    import zlib

    import numpy as np

    out = dict(_drawn_inputs(seed))
    spreads = {'L0_tok_b': (0.0, 0.1)}
    factors = {'L0_ffn_in_bias': 3.692}
    for name, (base, spread) in spreads.items():
        noise = np.random.default_rng([zlib.crc32(name.encode()), seed]).standard_normal(out[name].shape)
        drawn = base * np.exp(spread * noise) if base else spread * noise
        out[name] = jnp.asarray(drawn.astype(out[name].dtype))
    for name, factor in factors.items():
        out[name] = (out[name] * factor).astype(out[name].dtype)
    return out
```

```python
from contextlib import ExitStack

import numpy as np

import concourse.bass as bass
from concourse import mybir
from concourse.alu_op_type import AluOpType as ALU

F32 = mybir.dt.float32
F32R = mybir.dt.float32r
ACT = mybir.ActivationFunctionType
AX_X = mybir.AxisListType.X
P = 128

IMAGES, SIDE, CHANNELS, PATCH = 64, 96, 3, 16
GRID = SIDE // PATCH
PATCHES = GRID * GRID
TEXT = 32
SEQ = PATCHES + TEXT
DIM, HEADS = 192, 12
DH = DIM // HEADS
FEAT = 64
PATCH_DIM = PATCH * PATCH * CHANNELS
KC = PATCH_DIM // P
HID = 768
HC = HID // P
LN_EPS = 1e-5
KERNEL_EPS = 1e-4
REST = DIM - P
PAIRS = HEADS // 2
HALF = DIM // 2
VW = DH + 1
QUAD = 32

G = 4
GROUPS = IMAGES // G
GT = G * SEQ

EMB_TOK = 256
EMB_ITERS = IMAGES * PATCHES // EMB_TOK
SUB = EMB_TOK // P
N_PER_TILE = P // IMAGES

FT = 256
F_ITERS = IMAGES * SEQ // FT


def split_passes(hi0, lo0, hi1, lo1, x_hi0, x_lo0, x_st1):
    return [(hi0, x_hi0), (lo0, x_hi0), (hi0, x_lo0), (hi1, x_st1), (lo1, x_st1[0:REST])]


def ge(eng, semaphore, value):
    if not isinstance(value, int) or value > 0:
        eng.wait_ge(semaphore, value)


def embed_phase(nc, x_tiles, tok_w, tok_b, txt, tokens):
    with ExitStack() as ctx:
        def sb(name, shape, dt=F32):
            return ctx.enter_context(nc.sbuf_tensor(name, shape, dt))

        def sem(name):
            return ctx.enter_context(nc.semaphore(name))

        raw = sb("emb_raw", [P, EMB_ITERS, KC, EMB_TOK])
        w_raw = sb("emb_w_raw", [P, KC, DIM])
        w_hi = sb("emb_w_hi", [P, KC, DIM], F32R)
        w_lo = sb("emb_w_lo", [P, KC, DIM], F32R)
        bias = sb("emb_bias", [P, DIM])
        x_hi = sb("emb_x_hi", [P, SUB, KC, P], F32R)
        x_lo = sb("emb_x_lo", [P, SUB, KC, P], F32R)
        emb = sb("emb_out", [P, SUB, DIM])
        acc = [ctx.enter_context(nc.psum_tensor(f"emb_acc{s}", [P, 512], F32)) for s in range(SUB)]

        weights_in = sem("emb_weights_in")
        all_loaded = sem("emb_all_loaded")
        text_done = sem("emb_text_done")
        w_split = sem("emb_w_split")
        hi_done = [sem(f"emb_hi{s}") for s in range(SUB)]
        lo_done = [sem(f"emb_lo{s}") for s in range(SUB)]
        mm_done = [sem(f"emb_mm{s}") for s in range(SUB)]
        out_done = [sem(f"emb_out_done{s}") for s in range(SUB)]
        stored = [sem(f"emb_stored{s}") for s in range(SUB)]
        block = ctx.enter_context(nc.Block())

        def loop(eng, emit):
            emit(0)
            with eng.Fori(1, EMB_ITERS) as t:
                emit(t)

        @block.sync
        def _(sp):
            sp.dma_start(w_raw[:], tok_w.rearrange("(c p) n -> p c n", p=P)).then_inc(weights_in, 16)
            sp.dma_start(bias[:], tok_b.unsqueeze(0).to_broadcast([P, DIM])).then_inc(weights_in, 16)
            for t in range(EMB_ITERS):
                sp.dma_start(raw[:, t], x_tiles[t]).then_inc(all_loaded, 16)
                sp.wait_ge(all_loaded, 16 * (t + 1))
            sp.dma_start(tokens[:, PATCHES:SEQ, :], txt).then_inc(text_done, 16)
            sp.wait_ge(text_done, 16)

        @block.scalar
        def _(act):
            def emit(t):
                ge(act, all_loaded, 16 * t + 16)
                for s in range(SUB):
                    ge(act, mm_done[s], t)
                    nc.scalar.activation(x_hi[:, s], raw[:, t, :, s * P:(s + 1) * P],
                                         ACT.Copy).then_inc(hi_done[s], 1)

            loop(act, emit)

        @block.vector
        def _(dve):
            dve.wait_ge(weights_in, 32)
            nc.vector.tensor_copy(w_hi[:], w_raw[:]).then_inc(w_split, 1)
            dve.wait_ge(w_split, 1)
            nc.vector.tensor_tensor(w_lo[:], w_raw[:], w_hi[:].bitcast(F32), ALU.subtract).then_inc(w_split, 1)

            def emit(t):
                for s in range(SUB):
                    ge(dve, hi_done[s], t + 1)
                    ge(dve, mm_done[s], t)
                    nc.vector.tensor_tensor(x_lo[:, s], raw[:, t, :, s * P:(s + 1) * P],
                                            x_hi[:, s].bitcast(F32), ALU.subtract).then_inc(lo_done[s], 1)
                for s in range(SUB):
                    ge(dve, mm_done[s], t + 1)
                    ge(dve, stored[s], 16 * N_PER_TILE * t)
                    nc.vector.tensor_tensor(emb[:, s], acc[s][:, 0:DIM], bias[:],
                                            ALU.add).then_inc(out_done[s], 1)

            loop(dve, emit)

        @block.tensor
        def _(pe):
            pe.wait_ge(w_split, 2)

            def emit(t):
                for s in range(SUB):
                    ge(pe, lo_done[s], t + 1)
                    ge(pe, out_done[s], t)
                    for c in range(KC):
                        for n, (x, w) in enumerate(((x_hi, w_hi), (x_hi, w_lo), (x_lo, w_hi))):
                            last = nc.tensor.matmul(acc[s][:, 0:DIM], x[:, s, c], w[:, c],
                                                    start=(c == 0 and n == 0), stop=(c == KC - 1 and n == 2))
                    last.then_inc(mm_done[s], 1)

            loop(pe, emit)

        @block.gpsimd
        def _(pool):
            def emit(t):
                for s in range(SUB):
                    ge(pool, out_done[s], t + 1)
                    for n in range(N_PER_TILE):
                        pool.dma_start(tokens[:, bass.ds(t * (SUB * N_PER_TILE) + (s * N_PER_TILE + n), 1), :],
                                       emb[n * IMAGES:(n + 1) * IMAGES, s:s + 1]).then_inc(stored[s], 16)

            loop(pool, emit)
            for s in range(SUB):
                pool.wait_ge(stored[s], 16 * N_PER_TILE * EMB_ITERS)


def attention_phase(nc, tokens, w_all, proj_t, mixed):
    with ExitStack() as ctx:
        def sb(name, shape, dt=F32):
            return ctx.enter_context(nc.sbuf_tensor(name, shape, dt))

        def ps(name, shape):
            return ctx.enter_context(nc.psum_tensor(name, shape, F32))

        def sem(name):
            return ctx.enter_context(nc.semaphore(name))

        w0_raw = sb("w0_raw", [P, 4 * DIM])
        w1_raw = sb("w1_raw", [P, 4 * DIM])
        w0_hi = sb("w0_hi", [P, 4 * DIM], F32R)
        w0_lo = sb("w0_lo", [P, 4 * DIM], F32R)
        w1_hi = sb("w1_hi", [P, 4 * DIM], F32R)
        w1_lo = sb("w1_lo", [P, 4 * DIM], F32R)
        ident = sb("ident", [P, P])
        proj_raw = sb("proj_raw", [QUAD, P])
        proj_sc = sb("proj_sc", [QUAD, P])
        proj_st = sb("proj_st", [3 * QUAD, P], F32R)
        sel_raw = sb("sel_raw", [HEADS, HEADS * FEAT])
        sel = sb("sel", [QUAD + HEADS, HEADS * FEAT], F32R)
        diag_w = sb("diag_w", [HALF, HEADS // 2])
        eps_tile = sb("eps_tile", [P, 1])
        pow_tile = sb("pow_tile", [SEQ, G])
        ln_eps = sb("ln_eps", [SEQ, G])

        h_in = sb("h_in", [SEQ, G, DIM])
        bn_st = sb("bn_st", [SEQ, G, 6])
        bn_mv = sb("bn_mv", [SEQ, G, 2])
        var_eps = sb("var_eps", [SEQ, G])
        rstd = sb("rstd", [SEQ, G])
        carrier = sb("carrier", [1, 1])
        xn = sb("xn", [SEQ, G, DIM])
        xt0 = sb("xt0", [P, 2, GT], F32R)
        xt1 = sb("xt1", [P, GT], F32R)
        qk_hi = sb("qk_hi", [HALF, 4, GT], F32R)
        qk_lo = sb("qk_lo", [HALF, 4, GT], F32R)
        qk_sq = sb("qk_sq", [HALF, 4, GT])
        stack = sb("stack", [3 * QUAD, 4, 3, GT], F32R)
        v_aug = sb("v_aug", [SEQ, G, HEADS, VW])
        max_q = sb("max_q", [SEQ, G, HEADS])
        bounds = sb("bounds", [SEQ, G, 3 * QUAD])
        stab_k = sb("stab_k", [P, G])
        bound_k = sb("bound_k", [HEADS, G, SEQ])
        nb_q = sb("nb_q", [QUAD + HEADS, GT], F32R)
        nb_k = sb("nb_k", [QUAD + HEADS, GT], F32R)
        qp = sb("qp", [P, PAIRS, GT])
        kp = sb("kp", [SEQ, G, HEADS * FEAT])
        context = sb("context", [P, G, PAIRS, 2 * VW])
        den = sb("den", [SEQ, G, HEADS])
        attn = sb("attn", [SEQ, G, DIM])
        ot0 = sb("ot0", [P, 2, GT], F32R)
        ot1 = sb("ot1", [P, GT], F32R)
        h_res = sb("h_res", [SEQ, G, DIM])
        h_out = sb("h_out", [SEQ, G, DIM])

        tr_a = ps("tr_a", [P, 512])
        tr_b = ps("tr_b", [P, 512])
        pj = [ps("pj0", [P, 512]), ps("pj1", [P, 512])]
        wide = ps("wide", [P, 4, 512])

        const_in = sem("const_in")
        const_chain = sem("const_chain")
        const_w = sem("const_w")
        const_pool = sem("const_pool")
        h_loaded = sem("h_loaded")
        stats = sem("stats")
        moments = sem("moments")
        var_ready = sem("var_ready")
        rstd_ready = sem("rstd_ready")
        xn_ready = sem("xn_ready")
        x_transposed = sem("x_transposed")
        xt_hi = sem("xt_hi")
        xt_lo = sem("xt_lo")
        qk_mm = sem("qk_mm")
        qk_hi_ready = sem("qk_hi_ready")
        qk_sq_ready = sem("qk_sq_ready")
        qk_lo_ready = sem("qk_lo_ready")
        stacked = sem("stacked")
        v_mm = sem("v_mm")
        v_ready = sem("v_ready")
        dash_mm = sem("dash_mm")
        maxed = sem("maxed")
        diag_mm = sem("diag_mm")
        bounds_ready = sem("bounds_ready")
        bounds_tr = sem("bounds_tr")
        nb_ready = sem("nb_ready")
        fq_mm = sem("fq_mm")
        fk_mm = sem("fk_mm")
        qp_exp = sem("qp_exp")
        kp_exp = sem("kp_exp")
        qp_ready = sem("qp_ready")
        kp_ready = sem("kp_ready")
        ctx_mm = sem("ctx_mm")
        ctx_ready = sem("ctx_ready")
        att_mm = sem("att_mm")
        den_ready = sem("den_ready")
        attn_ready = sem("attn_ready")
        o_transposed = sem("o_transposed")
        ot_hi = sem("ot_hi")
        ot_lo = sem("ot_lo")
        wo_mm = sem("wo_mm")
        res_loaded = sem("res_loaded")
        res_ready = sem("res_ready")
        h_stored = sem("h_stored")
        block = ctx.enter_context(nc.Block())

        def tok(b):
            return slice(b * SEQ, (b + 1) * SEQ)

        def passes(c0, c1, x0, x1, t):
            return split_passes(w0_hi[:, c0:c1], w0_lo[:, c0:c1], w1_hi[:, c0:c1], w1_lo[0:REST, c0:c1],
                                x0[:, 0, t], x0[:, 1, t], x1[:, t])

        def pipeline(eng, emit):
            emit(0, False, True, True)
            emit(1, True, True, True)
            with eng.Fori(2, GROUPS - 1) as i:
                emit(i, True, True, True)
            emit(GROUPS - 1, True, True, False)
            emit(GROUPS, True, False, False)

        @block.sync
        def _(sp):
            sp.dma_start(w0_raw[:], w_all[0:P, :]).then_inc(const_in, 16)
            sp.dma_start(w1_raw[0:REST], w_all[P:DIM, :]).then_inc(const_in, 16)
            sp.dma_start(w1_raw[REST:P], w_all[P:DIM, :]).then_inc(const_in, 16)
            sp.wait_ge(const_pool, 1)
            for r in range(2):
                sp.dma_start(proj_raw[r * DH:(r + 1) * DH, r * FEAT:(r + 1) * FEAT], proj_t).then_inc(const_in, 16)

            def load(g):
                ge(sp, xn_ready, G * g)
                sp.dma_start(h_in[:], tokens[bass.ds(g * G, G)].rearrange("b s d -> s b d")).then_inc(h_loaded, 16)

            load(0)

            def emit(i, prev, cur, nxt):
                if nxt:
                    load(i + 1)
                if cur:
                    ge(sp, fk_mm, G * i)
                    ge(sp, qk_hi_ready, G * (i + 1))
                    for j in range(3):
                        for row in (0, 2):
                            sp.dma_start(stack[row * QUAD:(row + 1) * QUAD, :, j].bitcast(F32),
                                         qk_hi[j * QUAD:(j + 1) * QUAD].bitcast(F32)).then_inc(stacked, 16)
                    ge(sp, qk_lo_ready, G * (i + 1))
                    for j in range(3):
                        sp.dma_start(stack[QUAD:2 * QUAD, :, j].bitcast(F32),
                                     qk_lo[j * QUAD:(j + 1) * QUAD].bitcast(F32)).then_inc(stacked, 16)
                if prev:
                    g = i - 1
                    ge(sp, res_ready, G * g)
                    sp.dma_start(h_res[:], tokens[bass.ds(g * G, G)].rearrange("b s d -> s b d")
                                 ).then_inc(res_loaded, 16)
                    ge(sp, res_ready, G * (g + 1))
                    sp.dma_start(mixed[bass.ds(g * G, G)].rearrange("b s d -> s b d"), h_out[:]
                                 ).then_inc(h_stored, 16)

            pipeline(sp, emit)
            sp.wait_ge(h_stored, 16 * GROUPS)

        @block.gpsimd
        def _(pool):
            nc.gpsimd.memset(proj_raw[:], 0.0).then_inc(const_pool, 1)
            nc.gpsimd.memset(ident[:], 1.0).then_inc(const_chain, 1)
            nc.gpsimd.memset(sel_raw[:], -1.0).then_inc(const_chain, 1)
            nc.gpsimd.memset(diag_w[:], 0.5 * DH ** -0.5).then_inc(const_chain, 1)
            nc.gpsimd.memset(eps_tile[:], KERNEL_EPS).then_inc(const_chain, 1)
            nc.gpsimd.memset(pow_tile[:], -0.5).then_inc(const_chain, 1)
            nc.gpsimd.memset(ln_eps[:], LN_EPS).then_inc(const_chain, 1)
            nc.gpsimd.memset(v_aug[:], 1.0).then_inc(const_pool, 1)
            nc.gpsimd.memset(context[:], 0.0).then_inc(const_pool, 1)
            nc.gpsimd.memset(bounds[:], 0.0).then_inc(const_pool, 1)
            nc.gpsimd.memset(sel[:].bitcast(F32), 0.0).then_inc(const_pool, 1)
            nc.gpsimd.memset(nb_q[:].bitcast(F32), 0.0).then_inc(const_pool, 1)
            nc.gpsimd.memset(nb_k[:].bitcast(F32), 0.0).then_inc(const_pool, 1)
            pool.wait_ge(const_chain, 6)
            nc.gpsimd.affine_select(out=ident[:], in_=ident[:], compare_op=ALU.is_equal, fill=0.0,
                                    base=0, pattern=[[-1, P]], channel_multiplier=1).then_inc(const_pool, 1)
            nc.gpsimd.affine_select(out=sel_raw[:], in_=sel_raw[:], compare_op=ALU.is_ge, fill=0.0,
                                    base=0, pattern=[[1, HEADS * FEAT]],
                                    channel_multiplier=-FEAT).then_inc(const_chain, 1)
            nc.gpsimd.affine_select(out=diag_w[:], in_=diag_w[:], compare_op=ALU.is_ge, fill=0.0,
                                    base=0, pattern=[[-DH, HEADS // 2]], channel_multiplier=1).then_inc(const_chain, 1)
            pool.wait_ge(const_chain, 8)
            nc.gpsimd.affine_select(out=sel_raw[:], in_=sel_raw[:], compare_op=ALU.is_ge, fill=0.0,
                                    base=FEAT - 1, pattern=[[-1, HEADS * FEAT]],
                                    channel_multiplier=FEAT).then_inc(const_pool, 1)
            nc.gpsimd.affine_select(out=diag_w[:], in_=diag_w[:], compare_op=ALU.is_ge, fill=0.0,
                                    base=DH - 1, pattern=[[DH, HEADS // 2]],
                                    channel_multiplier=-1).then_inc(const_pool, 1)

            def norm(g):
                ge(pool, moments, G * (g + 1))
                ge(pool, xn_ready, G * g)
                nc.gpsimd.tensor_tensor(var_eps[:], bn_mv[:, :, 1], ln_eps[:], ALU.add).then_inc(var_ready, 1)
                ge(pool, var_ready, g + 1)
                nc.gpsimd.tensor_tensor(rstd[:], var_eps[:], pow_tile[:], ALU.pow).then_inc(rstd_ready, 1)

            norm(0)

            def emit(i, prev, cur, nxt):
                if nxt:
                    norm(i + 1)
                if cur:
                    for p in range(PAIRS):
                        ge(pool, qp_exp, PAIRS * i + p + 1)
                        nc.gpsimd.tensor_tensor(qp[:, p], qp[:, p], eps_tile[:].to_broadcast([P, GT]),
                                                ALU.add).then_inc(qp_ready, 1)
                    for b in range(G):
                        ge(pool, kp_exp, G * i + b + 1)
                        nc.gpsimd.tensor_tensor(kp[:, b], kp[:, b],
                                                eps_tile[0:SEQ].to_broadcast([SEQ, HEADS * FEAT]),
                                                ALU.add).then_inc(kp_ready, 1)

            pipeline(pool, emit)

        @block.scalar
        def _(act):
            def emit(i, prev, cur, nxt):
                g = i - 1
                if cur:
                    ge(act, v_mm, G * i)
                    ge(act, x_transposed, 2 * i + 1)
                    nc.scalar.activation(xt0[:, 0], tr_a[:, 0:GT], ACT.Copy).then_inc(xt_hi, 1)
                    ge(act, x_transposed, 2 * i + 2)
                    nc.scalar.activation(xt1[0:REST], tr_b[0:REST, 0:GT], ACT.Copy).then_inc(xt_hi, 1)
                    ge(act, stacked, 16 * 9 * i)
                    ge(act, diag_mm, i)
                    for c in range(4):
                        ge(act, qk_mm, 4 * i + c + 1)
                        nc.scalar.activation(qk_hi[:, c], pj[c % 2][0:HALF, 0:GT],
                                             ACT.Copy).then_inc(qk_hi_ready, 1)
                        nc.scalar.activation(qk_sq[:, c], pj[c % 2][0:HALF, 0:GT],
                                             ACT.Square).then_inc(qk_sq_ready, 1)
                if prev:
                    ge(act, ctx_mm, G * (g + 1))
                    ge(act, att_mm, G * g)
                    if isinstance(i, int) and i == 1:
                        act.wait_ge(const_pool, 3)
                    for r in range(2):
                        rows, cols = slice(r * FEAT, (r + 1) * FEAT), slice(r * VW, (r + 1) * VW)
                        nc.scalar.activation(
                            context[rows, :, :, cols],
                            wide[rows, :, 0:PAIRS * 2 * VW].rearrange("p b (q c) -> p b q c", q=PAIRS)[:, :, :, cols],
                            ACT.Copy).then_inc(ctx_ready, 1)
                if cur:
                    if not prev:
                        act.wait_ge(const_pool, 9)
                    for b in range(G):
                        ge(act, v_mm, G * i + b + 1)
                        nc.scalar.activation(v_aug[:, b, :, 0:DH],
                                             pj[b % 2][0:SEQ, 0:DIM].rearrange("p (h d) -> p h d", h=HEADS),
                                             ACT.Copy).then_inc(v_ready, 1)
                if prev:
                    ge(act, wo_mm, G * g)
                    ge(act, o_transposed, 2 * g + 1)
                    nc.scalar.activation(ot0[:, 0], pj[0][:, 0:GT], ACT.Copy).then_inc(ot_hi, 1)
                    ge(act, o_transposed, 2 * g + 2)
                    nc.scalar.activation(ot1[0:REST], pj[1][0:REST, 0:GT], ACT.Copy).then_inc(ot_hi, 1)
                if cur:
                    ge(act, att_mm, G * i)
                    for p in range(PAIRS):
                        ge(act, fq_mm, PAIRS * i + p + 1)
                        nc.scalar.activation(qp[:, p], wide[:, p % 4, 0:GT], ACT.Exp).then_inc(qp_exp, 1)
                    ge(act, ctx_mm, G * i)
                    for b in range(G):
                        ge(act, fk_mm, G * i + b + 1)
                        w = 2 * (b % 2)
                        nc.scalar.activation(kp[:, b].rearrange("p (a c) -> p a c", a=2),
                                             wide[0:SEQ, w:w + 2, 0:3 * P], ACT.Exp).then_inc(kp_exp, 1)

            pipeline(act, emit)

        @block.vector
        def _(dve):
            step = [0]

            def chained(ins):
                step[0] += 1
                ins.then_inc(const_w, 1)
                dve.wait_ge(const_w, step[0])

            dve.wait_ge(const_in, 16 * 5)
            chained(nc.vector.tensor_copy(w0_hi[:], w0_raw[:]))
            chained(nc.vector.tensor_copy(w1_hi[:], w1_raw[:]))
            chained(nc.vector.tensor_tensor(w0_lo[:], w0_raw[:], w0_hi[:].bitcast(F32), ALU.subtract))
            chained(nc.vector.tensor_tensor(w1_lo[:], w1_raw[:], w1_hi[:].bitcast(F32), ALU.subtract))
            chained(nc.vector.tensor_scalar(proj_sc[:], proj_raw[:], DH ** -0.25, None, ALU.mult))
            chained(nc.vector.tensor_copy(proj_st[0:QUAD], proj_sc[:]))
            chained(nc.vector.tensor_copy(proj_st[QUAD:2 * QUAD], proj_sc[:]))
            chained(nc.vector.tensor_tensor(proj_st[2 * QUAD:3 * QUAD], proj_sc[:],
                                            proj_st[0:QUAD].bitcast(F32), ALU.subtract))
            dve.wait_ge(const_pool, 10)
            chained(nc.vector.tensor_copy(sel[0:HEADS], sel_raw[:]))
            chained(nc.vector.tensor_copy(sel[QUAD:QUAD + HEADS], sel_raw[:]))

            def norm(g):
                ge(dve, h_loaded, 16 * (g + 1))
                for b in range(G):
                    nc.vector.bn_stats(bn_st[:, b], h_in[:, b]).then_inc(stats, 1)
                ge(dve, stats, G * (g + 1))
                nc.vector.memset(carrier[:], 0.0)
                for b in range(G):
                    nc.vector.bn_aggr(bn_mv[:, b], bn_st[:, b]).then_inc(moments, 1)
                ge(dve, rstd_ready, g + 1)
                ge(dve, x_transposed, 2 * g)
                for b in range(G):
                    nc.vector.tensor_scalar(xn[:, b], h_in[:, b], bn_mv[:, b, 0:1], rstd[:, b:b + 1],
                                            ALU.subtract, ALU.mult).then_inc(xn_ready, 1)

            norm(0)

            def emit(i, prev, cur, nxt):
                g = i - 1
                if cur:
                    ge(dve, xt_hi, 2 * i + 1)
                    nc.vector.tensor_tensor(xt0[:, 1], tr_a[:, 0:GT], xt0[:, 0].bitcast(F32),
                                            ALU.subtract).then_inc(xt_lo, 1)
                    ge(dve, xt_hi, 2 * i + 2)
                    nc.vector.tensor_tensor(xt1[REST:P], tr_b[0:REST, 0:GT], xt1[0:REST].bitcast(F32),
                                            ALU.subtract).then_inc(xt_lo, 1)
                    for c in range(4):
                        ge(dve, qk_sq_ready, 4 * i + c + 1)
                        nc.vector.tensor_tensor(qk_lo[:, c], pj[c % 2][0:HALF, 0:GT],
                                                qk_hi[:, c].bitcast(F32), ALU.subtract).then_inc(qk_lo_ready, 1)
                if prev:
                    ge(dve, att_mm, G * (g + 1))
                    ge(dve, attn_ready, G * g)
                    sums = wide[0:SEQ, :, 0:HEADS * VW].rearrange("p b (h c) -> p b h c", h=HEADS)
                    nc.vector.reciprocal(den[:], sums[:, :, :, DH]).then_inc(den_ready, 1)
                    ge(dve, den_ready, g + 1)
                    ge(dve, o_transposed, 2 * g)
                    for b in range(G):
                        nc.vector.tensor_tensor(attn[:, b].rearrange("p (h d) -> p h d", h=HEADS),
                                                sums[:, b, :, 0:DH],
                                                den[:, b].unsqueeze(2).to_broadcast([SEQ, HEADS, DH]),
                                                ALU.mult).then_inc(attn_ready, 1)
                if cur:
                    ge(dve, bounds_tr, i)
                    for b in range(G):
                        ge(dve, dash_mm, 8 * i + 2 * b + 1)
                        nc.vector.tensor_reduce(
                            max_q[:, b].rearrange("p (a h) -> p a h", a=2),
                            wide[0:SEQ, 0:2, 0:3 * P].rearrange("p a (h m) -> p a h m", m=FEAT),
                            AX_X, ALU.max).then_inc(maxed, 1)
                        ge(dve, dash_mm, 8 * i + 2 * b + 2)
                        nc.vector.tensor_reduce(
                            bounds[:, b, QUAD:QUAD + HEADS].rearrange("p (a h) -> p a h", a=2),
                            wide[0:SEQ, 2:4, 0:3 * P].rearrange("p a (h m) -> p a h m", m=FEAT),
                            AX_X, ALU.max).then_inc(maxed, 1)
                    ge(dve, diag_mm, i + 1)
                    ge(dve, maxed, 8 * i + 8)
                    diag = tr_b[0:SEQ, 0:G * 2 * HEADS].rearrange("p (b c) -> p b c", b=G)
                    nc.vector.tensor_tensor(bounds[:, :, 0:HEADS], diag[:, :, 0:HEADS], max_q[:],
                                            ALU.add).then_inc(bounds_ready, 1)
                    nc.vector.tensor_copy(bounds[:, :, 2 * QUAD:2 * QUAD + HEADS],
                                          diag[:, :, HEADS:2 * HEADS]).then_inc(bounds_ready, 1)
                    ge(dve, bounds_tr, i + 1)
                    ge(dve, nb_ready, 6 * i)
                    b_q, b_m, b_d = (tr_a[r * QUAD:r * QUAD + HEADS, 0:GT] for r in range(3))
                    st = stab_k[2 * QUAD:2 * QUAD + HEADS]
                    nc.vector.tensor_reduce(st, b_m.rearrange("p (b s) -> p b s", b=G), AX_X,
                                            ALU.max).then_inc(nb_ready, 1)
                    ge(dve, fq_mm, PAIRS * i)
                    nc.vector.tensor_copy(nb_q[0:HEADS], b_q).then_inc(nb_ready, 1)
                    ge(dve, nb_ready, 6 * i + 1)
                    nc.vector.tensor_tensor(bound_k[:], b_d.rearrange("p (b s) -> p b s", b=G),
                                            st.unsqueeze(2).to_broadcast([HEADS, G, SEQ]),
                                            ALU.add).then_inc(nb_ready, 1)
                    ge(dve, nb_ready, 6 * i + 2)
                    nc.vector.tensor_tensor(nb_q[QUAD:QUAD + HEADS], b_q, nb_q[0:HEADS].bitcast(F32),
                                            ALU.subtract).then_inc(nb_ready, 1)
                    ge(dve, nb_ready, 6 * i + 3)
                    ge(dve, fk_mm, G * i)
                    flat_k = bound_k[:].rearrange("p b s -> p (b s)")
                    nc.vector.tensor_copy(nb_k[0:HEADS], flat_k).then_inc(nb_ready, 1)
                    ge(dve, nb_ready, 6 * i + 5)
                    nc.vector.tensor_tensor(nb_k[QUAD:QUAD + HEADS], flat_k, nb_k[0:HEADS].bitcast(F32),
                                            ALU.subtract).then_inc(nb_ready, 1)
                if prev:
                    ge(dve, ot_hi, 2 * g + 1)
                    nc.vector.tensor_tensor(ot0[:, 1], pj[0][:, 0:GT], ot0[:, 0].bitcast(F32),
                                            ALU.subtract).then_inc(ot_lo, 1)
                    ge(dve, ot_hi, 2 * g + 2)
                    nc.vector.tensor_tensor(ot1[REST:P], pj[1][0:REST, 0:GT], ot1[0:REST].bitcast(F32),
                                            ALU.subtract).then_inc(ot_lo, 1)
                if nxt:
                    norm(i + 1)
                if prev:
                    ge(dve, res_loaded, 16 * (g + 1))
                    ge(dve, h_stored, 16 * g)
                    for b in range(G):
                        ge(dve, wo_mm, G * g + b + 1)
                        nc.vector.tensor_tensor(h_out[:, b], pj[b % 2][0:SEQ, 0:DIM], h_res[:, b],
                                                ALU.add).then_inc(res_ready, 1)

            pipeline(dve, emit)

        @block.tensor
        def _(pe):
            pe.wait_ge(const_w, 10)
            pe.wait_ge(const_pool, 10)

            def emit(i, prev, cur, nxt):
                g = i - 1
                if cur:
                    ge(pe, xn_ready, G * (i + 1))
                    for b in range(G):
                        last = nc.tensor.transpose(tr_a[:, tok(b)], xn[:, b, 0:P], ident[0:SEQ, 0:SEQ])
                    last.then_inc(x_transposed, 1)
                    for b in range(G):
                        last = nc.tensor.transpose(tr_b[0:REST, tok(b)], xn[:, b, P:DIM], ident[0:SEQ, 0:SEQ])
                    last.then_inc(x_transposed, 1)
                    ge(pe, xt_lo, 2 * (i + 1))
                    for c in range(4):
                        if c < 2:
                            ge(pe, res_ready, G * (i - 1) if prev else 0)
                        else:
                            ge(pe, qk_lo_ready, 4 * i + c - 1)
                        ps5 = passes(c * HALF, (c + 1) * HALF, xt0, xt1, slice(0, GT))
                        for n, (w, x) in enumerate(ps5):
                            last = nc.tensor.matmul(pj[c % 2][0:HALF, 0:GT], w, x, start=(n == 0), stop=(n == 4))
                        last.then_inc(qk_mm, 1)
                if prev:
                    ge(pe, kp_ready, G * (g + 1))
                    for b in range(G):
                        for p in range(PAIRS):
                            cols = slice(p * 2 * VW, (p + 1) * 2 * VW)
                            last = nc.tensor.matmul(
                                wide[:, b, cols], kp[:, b, p * P:(p + 1) * P],
                                v_aug[:, b, 2 * p:2 * p + 2].rearrange("p h d -> p (h d)"), start=True, stop=True)
                        last.then_inc(ctx_mm, 1)
                if cur:
                    for b in range(G):
                        if b < 2:
                            ge(pe, qk_lo_ready, 4 * i + b + 3)
                        else:
                            ge(pe, v_ready, G * i + b - 1)
                        ps5 = passes(2 * DIM, 3 * DIM, xt0, xt1, tok(b))
                        for n, (w, x) in enumerate(ps5):
                            last = nc.tensor.matmul(pj[b % 2][0:SEQ, 0:DIM], x, w, start=(n == 0), stop=(n == 4))
                        last.then_inc(v_mm, 1)
                if prev:
                    ge(pe, ctx_ready, 2 * (g + 1))
                    ge(pe, qp_ready, PAIRS * (g + 1))
                    for b in range(G):
                        for p in range(PAIRS):
                            last = nc.tensor.matmul(wide[0:SEQ, b, p * 2 * VW:(p + 1) * 2 * VW],
                                                    qp[:, p, tok(b)], context[:, b, p], start=True, stop=True)
                        last.then_inc(att_mm, 1)
                if cur:
                    ge(pe, qk_sq_ready, 4 * (i + 1))
                    for b in range(G):
                        for c in range(4):
                            o = b * 2 * HEADS + c * (HEADS // 2)
                            last = nc.tensor.matmul(tr_b[0:SEQ, o:o + HEADS // 2], qk_sq[:, c, tok(b)], diag_w[:],
                                                    start=True, stop=True)
                    last.then_inc(diag_mm, 1)
                    ge(pe, stacked, 16 * 9 * (i + 1))
                    if prev:
                        ge(pe, attn_ready, G * (g + 1))
                    for b in range(G):
                        for t in range(2):
                            if b:
                                ge(pe, maxed, 8 * i + 2 * (b - 1) + t + 1)
                            for p in range(PAIRS):
                                c, j = 2 * t + p // 3, p % 3
                                last = nc.tensor.matmul(wide[0:SEQ, 2 * t + p // 3, j * P:(j + 1) * P],
                                                        stack[:, c, j, tok(b)], proj_st[:], start=True, stop=True)
                            last.then_inc(dash_mm, 1)
                if prev:
                    ge(pe, attn_ready, G * (g + 1))
                    if cur:
                        ge(pe, v_ready, G * (i + 1))
                    else:
                        ge(pe, res_ready, G * g)
                    for b in range(G):
                        last = nc.tensor.transpose(pj[0][:, tok(b)], attn[:, b, 0:P], ident[0:SEQ, 0:SEQ])
                    last.then_inc(o_transposed, 1)
                    for b in range(G):
                        last = nc.tensor.transpose(pj[1][0:REST, tok(b)], attn[:, b, P:DIM], ident[0:SEQ, 0:SEQ])
                    last.then_inc(o_transposed, 1)
                if cur:
                    ge(pe, bounds_ready, 2 * (i + 1))
                    for b in range(G):
                        last = nc.tensor.transpose(tr_a[0:3 * QUAD, tok(b)], bounds[:, b], ident[0:SEQ, 0:SEQ])
                    last.then_inc(bounds_tr, 1)
                if prev:
                    ge(pe, ot_lo, 2 * (g + 1))
                    for b in range(G):
                        if b >= 2:
                            ge(pe, res_ready, G * g + b - 1)
                        ps5 = passes(3 * DIM, 4 * DIM, ot0, ot1, tok(b))
                        for n, (w, x) in enumerate(ps5):
                            last = nc.tensor.matmul(pj[b % 2][0:SEQ, 0:DIM], x, w, start=(n == 0), stop=(n == 4))
                        last.then_inc(wo_mm, 1)
                if cur:
                    ge(pe, nb_ready, 6 * i + 4)
                    for p in range(PAIRS):
                        if p >= 4:
                            ge(pe, qp_exp, PAIRS * i + p - 3)
                        out = wide[:, p % 4, 0:GT]
                        nc.tensor.matmul(out, proj_st[:], stack[:, p // 3, p % 3], start=True, stop=False)
                        nc.tensor.matmul(out, sel[:, p * P:(p + 1) * P], nb_q[:], start=False,
                                         stop=True).then_inc(fq_mm, 1)
                    ge(pe, nb_ready, 6 * i + 6)
                    for b in range(G):
                        if b < 2:
                            ge(pe, qp_exp, PAIRS * i + PAIRS)
                        else:
                            ge(pe, kp_exp, G * i + b - 1)
                        w = 2 * (b % 2)
                        for a in range(2):
                            nc.tensor.matmul(wide[0:SEQ, w + a, 0:3 * P], nb_k[:, tok(b)],
                                             sel[:, a * 3 * P:(a + 1) * 3 * P], start=True, stop=False,
                                             skip_group_check=True)
                            for j in range(3):
                                last = nc.tensor.matmul(wide[0:SEQ, w + a, j * P:(j + 1) * P],
                                                        stack[:, 2 + a, j, tok(b)], proj_st[:],
                                                        start=False, stop=(j == 2), skip_group_check=True)
                        last.then_inc(fk_mm, 1)

            pipeline(pe, emit)


def ffn_phase(nc, mixed, w1_t, b1, w2, out):
    TT = FT // P
    with ExitStack() as ctx:
        def sb(name, shape, dt=F32):
            return ctx.enter_context(nc.sbuf_tensor(name, shape, dt))

        def ps(name, shape):
            return ctx.enter_context(nc.psum_tensor(name, shape, F32))

        def sem(name):
            return ctx.enter_context(nc.semaphore(name))

        w1a_raw = sb("w1a_raw", [P, HID])
        w1b_raw = sb("w1b_raw", [P, HID])
        w1a_hi = sb("w1a_hi", [P, HID], F32R)
        w1a_lo = sb("w1a_lo", [P, HID], F32R)
        w1b_hi = sb("w1b_hi", [P, HID], F32R)
        w1b_lo = sb("w1b_lo", [P, HID], F32R)
        w2_raw = sb("w2_raw", [P, HC, DIM])
        w2_hi = sb("w2_hi", [P, HC, DIM], F32R)
        w2_lo = sb("w2_lo", [P, HC, DIM], F32R)
        b1_sb = sb("b1_sb", [P, HC])
        ident = sb("f_ident", [P, P])
        pow_tile = sb("f_pow", [P, TT])
        ln_eps = sb("f_ln_eps", [P, TT])
        h_in = sb("f_h_in", [P, 2, TT, DIM])
        bn_st = sb("f_bn_st", [P, TT, 6])
        bn_mv = sb("f_bn_mv", [P, TT, 2])
        var_eps = sb("f_var_eps", [P, TT])
        rstd = sb("f_rstd", [P, TT])
        carrier = sb("f_carrier", [1, 1])
        xn = sb("f_xn", [P, TT, DIM])
        xt0 = sb("f_xt0", [P, 2, FT], F32R)
        xt1 = sb("f_xt1", [P, FT], F32R)
        hid = sb("f_hid", [P, HC, FT])
        hid_hi = sb("f_hid_hi", [P, HC, FT], F32R)
        hid_lo = sb("f_hid_lo", [P, HC, FT], F32R)
        h_res = sb("f_h_res", [P, TT, DIM])
        h_out = sb("f_h_out", [P, TT, DIM])

        tr = [ps("f_tr0", [P, 512]), ps("f_tr1", [P, 512])]
        up = [ps("f_up0", [P, 512]), ps("f_up1", [P, 512])]
        down = [ps("f_down0", [P, 512]), ps("f_down1", [P, 512])]

        weights_in = sem("f_weights_in")
        const_chain = sem("f_const_chain")
        const_pool = sem("f_const_pool")
        w_split = sem("f_w_split")
        h_loaded = sem("f_h_loaded")
        stats = sem("f_stats")
        moments = sem("f_moments")
        var_ready = sem("f_var_ready")
        rstd_ready = sem("f_rstd_ready")
        xn_ready = sem("f_xn_ready")
        x_transposed = sem("f_x_transposed")
        xt_hi = sem("f_xt_hi")
        xt_lo = sem("f_xt_lo")
        up_mm = sem("f_up_mm")
        gelu_done = sem("f_gelu_done")
        hid_hi_ready = sem("f_hid_hi_ready")
        hid_lo_ready = sem("f_hid_lo_ready")
        down_mm = sem("f_down_mm")
        res_loaded = sem("f_res_loaded")
        res_ready = sem("f_res_ready")
        stored = sem("f_stored")
        block = ctx.enter_context(nc.Block())

        rows_in = mixed.flatten_outer_dims()
        rows_out = out.flatten_outer_dims()

        def pipeline(eng, emit):
            emit(0, False, True, True)
            emit(1, True, True, True)
            with eng.Fori(2, F_ITERS - 1) as i:
                emit(i, True, True, True)
            emit(F_ITERS - 1, True, True, False)
            emit(F_ITERS, True, False, False)

        @block.sync
        def _(sp):
            def load(g):
                ge(sp, xn_ready, TT * g)
                sp.dma_start(h_in[:, 0], rows_in[bass.ds(g * FT, FT), :].rearrange("(a p) d -> p a d", p=P)
                             ).then_inc(h_loaded, 16)

            load(0)
            sp.dma_start(w1a_raw[:], w1_t[0:P, :]).then_inc(weights_in, 16)
            sp.dma_start(w1b_raw[0:REST], w1_t[P:DIM, :]).then_inc(weights_in, 16)
            sp.dma_start(w1b_raw[REST:P], w1_t[P:DIM, :]).then_inc(weights_in, 16)
            sp.dma_start(b1_sb[:], b1).then_inc(weights_in, 16)
            sp.dma_start(w2_raw[:], w2.rearrange("(c p) n -> p c n", p=P)).then_inc(weights_in, 16)

            def emit(i, prev, cur, nxt):
                if nxt:
                    load(i + 1)
                if prev:
                    g = i - 1
                    ge(sp, res_ready, TT * g)
                    sp.dma_start(h_res[:], rows_in[bass.ds(g * FT, FT), :].rearrange("(a p) d -> p a d", p=P)
                                 ).then_inc(res_loaded, 16)
                    ge(sp, res_ready, TT * (g + 1))
                    sp.dma_start(rows_out[bass.ds(g * FT, FT), :].rearrange("(a p) d -> p a d", p=P), h_out[:]
                                 ).then_inc(stored, 16)

            pipeline(sp, emit)
            sp.wait_ge(stored, 16 * F_ITERS)

        @block.gpsimd
        def _(pool):
            nc.gpsimd.memset(ident[:], 1.0).then_inc(const_chain, 1)
            nc.gpsimd.memset(pow_tile[:], -0.5).then_inc(const_chain, 1)
            nc.gpsimd.memset(ln_eps[:], LN_EPS).then_inc(const_chain, 1)
            pool.wait_ge(const_chain, 3)
            nc.gpsimd.affine_select(out=ident[:], in_=ident[:], compare_op=ALU.is_equal, fill=0.0,
                                    base=0, pattern=[[-1, P]], channel_multiplier=1).then_inc(const_pool, 1)

            def norm(g):
                ge(pool, moments, TT * (g + 1))
                ge(pool, xn_ready, TT * g)
                nc.gpsimd.tensor_tensor(var_eps[:], bn_mv[:, :, 1], ln_eps[:], ALU.add).then_inc(var_ready, 1)
                ge(pool, var_ready, g + 1)
                nc.gpsimd.tensor_tensor(rstd[:], var_eps[:], pow_tile[:], ALU.pow).then_inc(rstd_ready, 1)

            norm(0)

            def emit(i, prev, cur, nxt):
                if nxt:
                    norm(i + 1)

            pipeline(pool, emit)

        @block.scalar
        def _(act):
            def emit(i, prev, cur, nxt):
                if cur:
                    if not prev:
                        act.wait_ge(weights_in, 16 * 5)
                    ge(act, up_mm, HC * i)
                    ge(act, x_transposed, 2 * i + 1)
                    nc.scalar.activation(xt0[:, 0], tr[0][:, 0:FT], ACT.Copy).then_inc(xt_hi, 1)
                    ge(act, x_transposed, 2 * i + 2)
                    nc.scalar.activation(xt1[0:REST], tr[1][0:REST, 0:FT], ACT.Copy).then_inc(xt_hi, 1)
                    for c in range(HC):
                        ge(act, up_mm, HC * i + c + 1)
                        ge(act, hid_lo_ready, HC * (i - 1) + c + 1 if prev else 0)
                        nc.scalar.activation(hid[:, c], up[c % 2][:, 0:FT], ACT.Gelu,
                                             bias=b1_sb[:, c:c + 1]).then_inc(gelu_done, 1)

            pipeline(act, emit)

        @block.vector
        def _(dve):
            dve.wait_ge(weights_in, 16 * 5)
            nc.vector.tensor_copy(w1a_hi[:], w1a_raw[:]).then_inc(w_split, 1)
            nc.vector.tensor_copy(w1b_hi[:], w1b_raw[:]).then_inc(w_split, 1)
            nc.vector.tensor_copy(w2_hi[:], w2_raw[:]).then_inc(w_split, 1)
            dve.wait_ge(w_split, 3)
            nc.vector.tensor_tensor(w1a_lo[:], w1a_raw[:], w1a_hi[:].bitcast(F32), ALU.subtract).then_inc(w_split, 1)
            nc.vector.tensor_tensor(w1b_lo[:], w1b_raw[:], w1b_hi[:].bitcast(F32), ALU.subtract).then_inc(w_split, 1)
            nc.vector.tensor_tensor(w2_lo[:], w2_raw[:], w2_hi[:].bitcast(F32), ALU.subtract).then_inc(w_split, 1)

            def norm(g):
                ge(dve, h_loaded, 16 * (g + 1))
                for b in range(TT):
                    nc.vector.bn_stats(bn_st[:, b], h_in[:, 0, b]).then_inc(stats, 1)
                ge(dve, stats, TT * (g + 1))
                nc.vector.memset(carrier[:], 0.0)
                for b in range(TT):
                    nc.vector.bn_aggr(bn_mv[:, b], bn_st[:, b]).then_inc(moments, 1)
                ge(dve, rstd_ready, g + 1)
                ge(dve, x_transposed, 2 * g)
                for b in range(TT):
                    nc.vector.tensor_scalar(xn[:, b], h_in[:, 0, b], bn_mv[:, b, 0:1], rstd[:, b:b + 1],
                                            ALU.subtract, ALU.mult).then_inc(xn_ready, 1)

            norm(0)

            def emit(i, prev, cur, nxt):
                g = i - 1
                if cur:
                    ge(dve, xt_hi, 2 * i + 1)
                    nc.vector.tensor_tensor(xt0[:, 1], tr[0][:, 0:FT], xt0[:, 0].bitcast(F32),
                                            ALU.subtract).then_inc(xt_lo, 1)
                    ge(dve, xt_hi, 2 * i + 2)
                    nc.vector.tensor_tensor(xt1[REST:P], tr[1][0:REST, 0:FT], xt1[0:REST].bitcast(F32),
                                            ALU.subtract).then_inc(xt_lo, 1)
                    for c in range(HC):
                        ge(dve, gelu_done, HC * i + c + 1)
                        ge(dve, down_mm, HC * (i - 1) + c + 1 if prev else 0)
                        nc.vector.tensor_copy(hid_hi[:, c], hid[:, c]).then_inc(hid_hi_ready, 1)
                        ge(dve, hid_hi_ready, HC * i + c + 1)
                        nc.vector.tensor_tensor(hid_lo[:, c], hid[:, c], hid_hi[:, c].bitcast(F32),
                                                ALU.subtract).then_inc(hid_lo_ready, 1)
                if nxt:
                    norm(i + 1)
                if prev:
                    ge(dve, res_loaded, 16 * (g + 1))
                    ge(dve, stored, 16 * g)
                    ge(dve, down_mm, HC * (g + 1))
                    for b in range(TT):
                        nc.vector.tensor_tensor(h_out[:, b], down[b][:, 0:DIM], h_res[:, b],
                                                ALU.add).then_inc(res_ready, 1)

            pipeline(dve, emit)

        @block.tensor
        def _(pe):
            pe.wait_ge(w_split, 6)
            pe.wait_ge(const_pool, 1)

            def emit(i, prev, cur, nxt):
                g = i - 1
                if cur:
                    ge(pe, xn_ready, TT * (i + 1))
                    for b in range(TT):
                        last = nc.tensor.transpose(tr[0][:, b * P:(b + 1) * P], xn[:, b, 0:P], ident[:])
                    last.then_inc(x_transposed, 1)
                    for b in range(TT):
                        last = nc.tensor.transpose(tr[1][0:REST, b * P:(b + 1) * P], xn[:, b, P:DIM], ident[:])
                    last.then_inc(x_transposed, 1)
                for c in range(HC):
                    if prev:
                        if c == 0:
                            ge(pe, res_ready, TT * g)
                        ge(pe, hid_lo_ready, HC * g + c + 1)
                        for b in range(TT):
                            t = slice(b * P, (b + 1) * P)
                            for n, (x, w) in enumerate(((hid_hi, w2_hi), (hid_hi, w2_lo), (hid_lo, w2_hi))):
                                last = nc.tensor.matmul(down[b][:, 0:DIM], x[:, c, t], w[:, c],
                                                        start=(c == 0 and n == 0), stop=(c == HC - 1 and n == 2))
                        last.then_inc(down_mm, 1)
                    if cur:
                        if c == 0:
                            ge(pe, xt_lo, 2 * (i + 1))
                        if c >= 2:
                            ge(pe, gelu_done, HC * i + c - 1)
                        elif prev:
                            ge(pe, gelu_done, HC * i)
                        s = slice(c * P, (c + 1) * P)
                        ps5 = split_passes(w1a_hi[:, s], w1a_lo[:, s], w1b_hi[:, s], w1b_lo[0:REST, s],
                                           xt0[:, 0], xt0[:, 1], xt1[:])
                        for n, (w, x) in enumerate(ps5):
                            last = nc.tensor.matmul(up[c % 2][:, 0:FT], w, x, start=(n == 0), stop=(n == 4))
                        last.then_inc(up_mm, 1)

            pipeline(pe, emit)


def build_program(nc, x_tiles, txt, tok_w, tok_b, w_all, proj_t, w1_t, b1, w2, out):
    tokens = nc.dram_tensor("tokens", (IMAGES, SEQ, DIM), F32, kind="Internal").ap()
    mixed = nc.dram_tensor("mixed", (IMAGES, SEQ, DIM), F32, kind="Internal").ap()
    embed_phase(nc, x_tiles, tok_w, tok_b, txt, tokens)
    attention_phase(nc, tokens, w_all, proj_t, mixed)
    ffn_phase(nc, mixed, w1_t, b1, w2, out)


def kernel(**inputs):
    import concourse.bacc as bacc
    from concourse.bass_utils import run_bass_kernel_spmd

    a = {k: np.asarray(v) for k, v in inputs.items()}
    x = a["x"].reshape(IMAGES, GRID, PATCH, GRID, PATCH, CHANNELS).transpose(2, 4, 5, 1, 3, 0)
    x = x.reshape(KC, P, EMB_ITERS, EMB_TOK).transpose(2, 1, 0, 3)
    layout = {
        "x_tiles": x,
        "txt_in": a["txt"],
        "tok_w": a["L0_tok_W"],
        "tok_b": a["L0_tok_b"],
        "w_all": np.concatenate([a["L0_attn_Wq"], a["L0_attn_Wk"], a["L0_attn_Wv"], a["L0_attn_Wo"]], axis=1),
        "proj_t": a["L0_attn_proj"].T,
        "w1_t": a["L0_ffn_in_weight"].T,
        "b1": a["L0_ffn_in_bias"].reshape(HC, P).T,
        "w2": a["L0_ffn_out_weight"],
    }
    nc = bacc.Bacc("TRN2", target_bir_lowering=False, num_devices=1)
    arrays, args = {}, []
    for name, value in layout.items():
        arrays[name] = np.ascontiguousarray(value)
        args.append(nc.dram_tensor(name, arrays[name].shape, F32, kind="ExternalInput").ap())
    out = nc.dram_tensor("out", (IMAGES, SEQ, DIM), F32, kind="ExternalOutput").ap()
    build_program(nc, *args, out)
    result = run_bass_kernel_spmd(nc, [arrays], core_ids=[0])
    return result.results[0]["out"]
```

```python
from contextlib import ExitStack

import numpy as np

import concourse.bass as bass
from concourse import mybir
from concourse.alu_op_type import AluOpType as ALU

F32 = mybir.dt.float32
F32R = mybir.dt.float32r
ACT = mybir.ActivationFunctionType
AX_X = mybir.AxisListType.X
P = 128

IMAGES, SIDE, CHANNELS, PATCH = 64, 96, 3, 16
GRID = SIDE // PATCH
PATCHES = GRID * GRID
TEXT = 32
SEQ = PATCHES + TEXT
DIM, HEADS = 192, 12
DH = DIM // HEADS
FEAT = 64
PATCH_DIM = PATCH * PATCH * CHANNELS
KC = PATCH_DIM // P
HID = 768
HC = HID // P
LN_EPS = 1e-5
KERNEL_EPS = 1e-4
REST = DIM - P
PAIRS = HEADS // 2
HALF = DIM // 2
VW = DH + 1
QUAD = 32

G = 4
GROUPS = IMAGES // G
GT = G * SEQ

EMB_TILES = IMAGES * PATCHES // P
SUB = 2
LOADS = 3
BODY = SUB * LOADS
ROUNDS = EMB_TILES // BODY
RING = 3

FT = 256
F_ITERS = IMAGES * SEQ // FT


def split_passes(hi0, lo0, hi1, lo1, x_hi0, x_lo0, x_st1):
    return [(hi0, x_hi0), (lo0, x_hi0), (hi0, x_lo0), (hi1, x_st1), (lo1, x_st1[0:REST])]


def since(value):
    return max(value, 0) if isinstance(value, int) else value


class Weights:

    def __init__(self, nc, ctx):
        def sb(name, shape, dt=F32):
            return ctx.enter_context(nc.sbuf_tensor(name, shape, dt))

        self.w0_hi = sb("w0_hi", [P, 4 * DIM], F32R)
        self.w0_lo = sb("w0_lo", [P, 4 * DIM], F32R)
        self.w1_hi = sb("w1_hi", [P, 4 * DIM], F32R)
        self.w1_lo = sb("w1_lo", [P, 4 * DIM], F32R)
        self.proj_st = sb("proj_st", [3 * QUAD, P], F32R)
        self.sel = sb("sel", [P, HEADS * FEAT], F32R)
        self.diag_w = sb("diag_w", [HALF, QUAD])
        self.ident = sb("ident", [P, P])
        self.w1a_hi = sb("w1a_hi", [P, HID], F32R)
        self.w1a_lo = sb("w1a_lo", [P, HID], F32R)
        self.w1b_hi = sb("w1b_hi", [P, HID], F32R)
        self.w1b_lo = sb("w1b_lo", [P, HID], F32R)
        self.w2_parts = sb("w2_parts", [P, HC, 2, DIM], F32R)
        self.b1 = sb("b1_sb", [P, HC])


def embed_phase(nc, w, x_tiles, tok_w, tok_b, w_all, proj_t, w1_t, b1, w2, patches):
    with ExitStack() as ctx:
        def sb(name, shape, dt=F32):
            return ctx.enter_context(nc.sbuf_tensor(name, shape, dt))

        def sem(name):
            return ctx.enter_context(nc.semaphore(name))

        raw = sb("emb_raw", [P, LOADS, KC, SUB * P])
        w_raw = sb("emb_w_raw", [P, KC, DIM])
        w_parts = sb("emb_w_parts", [P, KC, 2, DIM], F32R)
        bias = sb("emb_bias", [P, DIM])
        x_hi = sb("emb_x_hi", [P, RING, KC, P], F32R)
        x_lo = sb("emb_x_lo", [P, RING, KC, P], F32R)
        part = sb("emb_part", [P, RING, DIM])
        emb = sb("emb_out", [P, RING, DIM])
        acc = [ctx.enter_context(nc.psum_tensor(f"emb_acc{s}", [P, 512], F32)) for s in range(RING)]

        w0_raw = sb("w0_raw", [P, 4 * DIM])
        w1_raw = sb("w1_raw", [P, 4 * DIM])
        w1a_raw = sb("w1a_raw", [P, HID])
        w1b_raw = sb("w1b_raw", [P, HID])
        w2_raw = sb("w2_raw", [P, HC, DIM])
        proj_raw = sb("proj_raw", [QUAD, P])
        proj_sc = sb("proj_sc", [QUAD, P])
        sel_raw = sb("sel_raw", [QUAD, HEADS // 2 * FEAT])

        tok_w_in = sem("emb_tok_w_in")
        loaded = [sem(f"emb_loaded{s}") for s in range(LOADS)]
        w_split = sem("emb_w_split")
        hi_done = sem("emb_hi_done")
        lo_done = sem("emb_lo_done")
        mm_done = sem("emb_mm_done")
        part_done = sem("emb_part_done")
        out_done = sem("emb_out_done")
        stored = [sem(f"emb_stored{s}") for s in range(RING)]
        weights_in = sem("weights_in")
        proj_cleared = sem("proj_cleared")
        fill = sem("fill")
        block = ctx.enter_context(nc.Block())

        def rounds(eng, emit):
            for u in range(BODY):
                emit(0, u)
            with eng.Fori(1, ROUNDS) as r:
                for u in range(BODY):
                    emit(r, u)

        @block.sync
        def _(sp):
            def load(n):
                sp.dma_start(raw[:, n], x_tiles[n]).then_inc(loaded[n], 16)

            load(0)
            sp.dma_start(w_raw[:], tok_w.rearrange("(c p) n -> p c n", p=P)).then_inc(tok_w_in, 16)
            sp.dma_start(bias[:], tok_b.unsqueeze(0).to_broadcast([P, DIM])).then_inc(tok_w_in, 16)
            for n in range(1, LOADS):
                load(n)
            sp.dma_start(w0_raw[:], w_all[0:P, :]).then_inc(weights_in, 16)
            sp.dma_start(w1_raw[0:REST], w_all[P:DIM, :]).then_inc(weights_in, 16)
            sp.dma_start(w1_raw[REST:P], w_all[P:DIM, :]).then_inc(weights_in, 16)
            sp.wait_ge(proj_cleared, 1)
            for r in range(2):
                sp.dma_start(proj_raw[r * DH:(r + 1) * DH, r * FEAT:(r + 1) * FEAT], proj_t).then_inc(weights_in, 16)
            sp.dma_start(w1a_raw[:], w1_t[0:P, :]).then_inc(weights_in, 16)
            sp.dma_start(w1b_raw[0:REST], w1_t[P:DIM, :]).then_inc(weights_in, 16)
            sp.dma_start(w1b_raw[REST:P], w1_t[P:DIM, :]).then_inc(weights_in, 16)
            sp.dma_start(w.b1[:], b1).then_inc(weights_in, 16)
            sp.dma_start(w2_raw[:], w2.rearrange("(c p) n -> p c n", p=P)).then_inc(weights_in, 16)

            def emit(r, u, more=True):
                t = r * BODY + u
                if u % SUB == 0 and more:
                    k = u // SUB
                    sp.wait_ge(lo_done, t + SUB)
                    sp.dma_start(raw[:, k], x_tiles[bass.ds(r * LOADS + (k + LOADS), 1)].squeeze(0)
                                 ).then_inc(loaded[k], 16)
                sp.wait_ge(out_done, t + 1)
                sp.dma_start(patches[bass.ds(t * P, P), :], emb[:, u % RING]).then_inc(stored[u % RING], 16)

            for u in range(BODY):
                emit(0, u)
            with sp.Fori(1, ROUNDS - 1) as r:
                for u in range(BODY):
                    emit(r, u)
            for u in range(BODY):
                emit(ROUNDS - 1, u, False)
            for s in range(RING):
                sp.wait_ge(stored[s], 16 * EMB_TILES // RING)

        @block.scalar
        def _(act):
            def emit(r, u):
                t = r * BODY + u
                n, s = u // SUB, u % SUB
                if s == 0:
                    act.wait_ge(loaded[n], 16 * (r + 1))
                act.wait_ge(mm_done, since(t - RING + 1))
                nc.scalar.activation(x_hi[:, u % RING], raw[:, n, :, s * P:(s + 1) * P],
                                     ACT.Copy).then_inc(hi_done, 1)

            rounds(act, emit)

        @block.vector
        def _(dve):
            dve.wait_ge(tok_w_in, 32)
            nc.vector.tensor_copy(w_parts[:, :, 0], w_raw[:]).then_inc(w_split, 1)
            dve.wait_ge(w_split, 1)
            nc.vector.tensor_tensor(w_parts[:, :, 1], w_raw[:], w_parts[:, :, 0].bitcast(F32),
                                    ALU.subtract).then_inc(w_split, 1)

            def low_part(r, u):
                t = r * BODY + u
                n, s = u // SUB, u % SUB
                dve.wait_ge(hi_done, t + 1)
                dve.wait_ge(mm_done, since(t - RING + 1))
                nc.vector.tensor_tensor(x_lo[:, u % RING], raw[:, n, :, s * P:(s + 1) * P],
                                        x_hi[:, u % RING].bitcast(F32), ALU.subtract).then_inc(lo_done, 1)

            def finish(r, u, t):
                s = u % RING
                dve.wait_ge(mm_done, t + 1)
                dve.wait_ge(out_done, since(t - RING + 1))
                nc.vector.tensor_tensor(part[:, s], acc[s][:, DIM:2 * DIM], bias[:], ALU.add).then_inc(part_done, 1)
                dve.wait_ge(part_done, t + 1)
                if not (isinstance(r, int) and r == 0):
                    dve.wait_ge(stored[s], 16 * (r * (BODY // RING) + u // RING))
                elif u >= RING:
                    dve.wait_ge(stored[s], 16 * (u // RING))
                nc.vector.tensor_tensor(emb[:, s], acc[s][:, 0:DIM], part[:, s], ALU.add).then_inc(out_done, 1)

            def emit(r, u):
                low_part(r, u)
                if u > 0:
                    finish(r, u - 1, r * BODY + u - 1)
                elif not isinstance(r, int):
                    finish(r - 1, BODY - 1, (r - 1) * BODY + BODY - 1)

            rounds(dve, emit)
            finish(ROUNDS - 1, BODY - 1, EMB_TILES - 1)

        @block.tensor
        def _(pe):
            pe.wait_ge(w_split, 2)

            def emit(r, u):
                t = r * BODY + u
                s = u % RING
                pe.wait_ge(lo_done, t + 1)
                pe.wait_ge(out_done, since(t - RING + 1))
                for c in range(KC):
                    nc.tensor.matmul(acc[s][:, 0:2 * DIM], x_hi[:, s, c],
                                     w_parts[:, c].rearrange("p k n -> p (k n)"),
                                     start=(c == 0), stop=False, skip_group_check=True)
                    last = nc.tensor.matmul(acc[s][:, 0:DIM], x_lo[:, s, c], w_parts[:, c, 0],
                                            start=False, stop=(c == KC - 1), skip_group_check=True)
                last.then_inc(mm_done, 1)

            rounds(pe, emit)

        @block.gpsimd
        def _(pool):
            step = [0]

            def chained(ins):
                step[0] += 1
                ins.then_inc(fill, 1)
                pool.wait_ge(fill, step[0])

            nc.gpsimd.memset(proj_raw[:], 0.0).then_inc(proj_cleared, 1)
            chained(nc.gpsimd.memset(w.ident[:], 1.0))
            chained(nc.gpsimd.memset(sel_raw[:], -1.0))
            chained(nc.gpsimd.memset(w.sel[:].bitcast(F32), 0.0))
            chained(nc.gpsimd.memset(w.diag_w[:], 0.5 * DH ** -0.5))
            chained(nc.gpsimd.affine_select(out=w.ident[:], in_=w.ident[:], compare_op=ALU.is_equal, fill=0.0,
                                            base=0, pattern=[[-1, P]], channel_multiplier=1))
            chained(nc.gpsimd.affine_select(out=sel_raw[:], in_=sel_raw[:], compare_op=ALU.is_ge, fill=0.0,
                                            base=0, pattern=[[1, HEADS // 2 * FEAT]],
                                            channel_multiplier=-FEAT))
            chained(nc.gpsimd.affine_select(out=w.diag_w[:], in_=w.diag_w[:], compare_op=ALU.is_ge, fill=0.0,
                                            base=0, pattern=[[-DH, QUAD]], channel_multiplier=1))
            chained(nc.gpsimd.affine_select(out=sel_raw[:], in_=sel_raw[:], compare_op=ALU.is_ge, fill=0.0,
                                            base=FEAT - 1, pattern=[[-1, HEADS // 2 * FEAT]],
                                            channel_multiplier=FEAT))
            chained(nc.gpsimd.affine_select(out=w.diag_w[:], in_=w.diag_w[:], compare_op=ALU.is_ge, fill=0.0,
                                            base=DH - 1, pattern=[[DH, QUAD]], channel_multiplier=-1))
            for n in range(P // QUAD):
                half = (n % 2) * (HEADS // 2) * FEAT
                chained(nc.gpsimd.tensor_copy(w.sel[n * QUAD:(n + 1) * QUAD, half:half + HEADS // 2 * FEAT],
                                              sel_raw[:]))
            pool.wait_ge(weights_in, 16 * 10)
            splits = ((w0_raw[:], w.w0_hi[:], w.w0_lo[:]), (w1_raw[:], w.w1_hi[:], w.w1_lo[:]),
                      (w1a_raw[:], w.w1a_hi[:], w.w1a_lo[:]), (w1b_raw[:], w.w1b_hi[:], w.w1b_lo[:]),
                      (w2_raw[:], w.w2_parts[:, :, 0], w.w2_parts[:, :, 1]))
            for value, hi, lo in splits:
                chained(nc.gpsimd.tensor_copy(hi, value))
            chained(nc.gpsimd.tensor_scalar(proj_sc[:], proj_raw[:], DH ** -0.25, None, ALU.mult))
            for value, hi, lo in splits:
                chained(nc.gpsimd.tensor_tensor(lo, value, hi.bitcast(F32), ALU.subtract))
            chained(nc.gpsimd.tensor_copy(w.proj_st[0:QUAD], proj_sc[:]))
            chained(nc.gpsimd.tensor_copy(w.proj_st[QUAD:2 * QUAD], proj_sc[:]))
            chained(nc.gpsimd.tensor_tensor(w.proj_st[2 * QUAD:3 * QUAD], proj_sc[:],
                                            w.proj_st[0:QUAD].bitcast(F32), ALU.subtract))

def attention_phase(nc, w, patches, txt, mixed):
    with ExitStack() as ctx:
        def sb(name, shape, dt=F32):
            return ctx.enter_context(nc.sbuf_tensor(name, shape, dt))

        def ps(name, shape):
            return ctx.enter_context(nc.psum_tensor(name, shape, F32))

        def sem(name):
            return ctx.enter_context(nc.semaphore(name))

        eps_tile = sb("eps_tile", [P, 1])
        pow_tile = sb("pow_tile", [SEQ, G])
        ln_eps = sb("ln_eps", [SEQ, G])

        h_in = sb("h_in", [SEQ, G, DIM])
        bn_st = sb("bn_st", [SEQ, G, 6])
        bn_mv = sb("bn_mv", [SEQ, G, 2])
        var_eps = sb("var_eps", [SEQ, G])
        rstd = sb("rstd", [SEQ, G])
        carrier = sb("carrier", [1, 1])
        xn = sb("xn", [SEQ, G, DIM])
        xt0 = sb("xt0", [P, 2, GT], F32R)
        xt1 = sb("xt1", [P, GT], F32R)
        qk_hi = sb("qk_hi", [HALF, 4, GT], F32R)
        qk_lo = sb("qk_lo", [HALF, 4, GT], F32R)
        qk_sq = [sb(f"qk_sq{s}", [HALF, 4, GT]) for s in range(2)]
        stack = [sb(f"stack{s}", [3 * QUAD, 3, 4, GT], F32R) for s in range(2)]
        v_aug = [sb(f"v_aug{s}", [SEQ, G, HEADS, VW]) for s in range(2)]
        bounds = sb("bounds", [SEQ, G, P])
        stab_k = sb("stab_k", [P, G])
        bound_k = sb("bound_k", [FEAT, G, SEQ])
        nb_q = sb("nb_q", [P, GT], F32R)
        nb_k = sb("nb_k", [P, GT], F32R)
        qp = sb("qp", [P, PAIRS, GT])
        kp = sb("kp", [SEQ, G, HEADS * FEAT])
        context = sb("context", [P, G, PAIRS, 2 * VW])
        den = sb("den", [SEQ, G, HEADS])
        attn = sb("attn", [SEQ, G, DIM])
        ot0 = sb("ot0", [P, 2, GT], F32R)
        ot1 = sb("ot1", [P, GT], F32R)
        h_res = sb("h_res", [SEQ, G, DIM])
        h_out = sb("h_out", [SEQ, G, DIM])

        tr = [ps("tr0", [P, 512]), ps("tr1", [P, 512])]
        pj_banks = ps("pj", [P, 2, 512])
        pj = [pj_banks[:, 0], pj_banks[:, 1]]
        wide = ps("wide", [P, 4, 512])

        const_pool = sem("const_pool")
        h_loaded = sem("h_loaded")
        stats = sem("stats")
        moments = sem("moments")
        var_ready = sem("var_ready")
        rstd_ready = sem("rstd_ready")
        xn_ready = sem("xn_ready")
        x_transposed = sem("x_transposed")
        xt_hi = sem("xt_hi")
        xt_lo = sem("xt_lo")
        qk_mm = sem("qk_mm")
        qk_hi_ready = sem("qk_hi_ready")
        qk_sq_ready = sem("qk_sq_ready")
        qk_lo_ready = sem("qk_lo_ready")
        stacked = sem("stacked")
        v_mm = sem("v_mm")
        v_ready = sem("v_ready")
        dash_mm = sem("dash_mm")
        maxed = sem("maxed")
        diag_mm = sem("diag_mm")
        bounds_tr = sem("bounds_tr")
        stab_ready = sem("stab_ready")
        bound_k_ready = sem("bound_k_ready")
        nbk_hi = sem("nbk_hi")
        nbk_ready = sem("nbk_ready")
        nbq_hi = sem("nbq_hi")
        nbq_ready = sem("nbq_ready")
        fq_mm = sem("fq_mm")
        fk_mm = sem("fk_mm")
        qp_exp = sem("qp_exp")
        kp_exp = sem("kp_exp")
        qp_ready = sem("qp_ready")
        kp01_ready = sem("kp01_ready")
        kp23_ready = sem("kp23_ready")
        ctx_mm = sem("ctx_mm")
        ctx_ready = sem("ctx_ready")
        att_mm = sem("att_mm")
        den_ready = sem("den_ready")
        attn_ready = sem("attn_ready")
        o_transposed = sem("o_transposed")
        ot_hi = sem("ot_hi")
        ot_lo = sem("ot_lo")
        wo_mm = sem("wo_mm")
        res_loaded = sem("res_loaded")
        res_ready = sem("res_ready")
        h_stored = sem("h_stored")
        block = ctx.enter_context(nc.Block())

        def tok(b):
            return slice(b * SEQ, (b + 1) * SEQ)

        def passes(c0, c1, x0, x1, t):
            return split_passes(w.w0_hi[:, c0:c1], w.w0_lo[:, c0:c1], w.w1_hi[:, c0:c1], w.w1_lo[0:REST, c0:c1],
                                x0[:, 0, t], x0[:, 1, t], x1[:, t])

        def feature_banks(b):
            return (wide[0:SEQ, 2:4], wide[0:SEQ, 0:2], pj_banks[0:SEQ], wide[0:SEQ, 2:4])[b][:, :, 0:3 * P]

        LOOP_FROM, LOOP_TO = 3, GROUPS - 3

        def pipeline(eng, emit):
            def single(i):
                emit(i, i % 2, [0 <= i + d < GROUPS for d in (-2, -1, 0, 1, 2)])

            for i in range(LOOP_FROM):
                single(i)
            with eng.Fori(LOOP_FROM, LOOP_TO - 1, 2) as i:
                emit(i, LOOP_FROM % 2, [True] * 5)
                emit(i + 1, (LOOP_FROM + 1) % 2, [True] * 5)
            for i in range(LOOP_TO, GROUPS + 2):
                single(i)

        patch_rows = patches.rearrange("(b n) d -> b n d", n=PATCHES)

        @block.sync
        def _(sp):
            def load_tokens(g, dst, done):
                sp.dma_start(dst[0:PATCHES], patch_rows[bass.ds(g * G, G)].rearrange("b s d -> s b d")
                             ).then_inc(done, 16)
                sp.dma_start(dst[PATCHES:SEQ], txt[bass.ds(g * G, G)].rearrange("b s d -> s b d")
                             ).then_inc(done, 16)

            def load(g):
                sp.wait_ge(xn_ready, since(G * g))
                load_tokens(g, h_in, h_loaded)

            def load_residual(g):
                sp.wait_ge(res_ready, since(G * g))
                load_tokens(g, h_res, res_loaded)

            def stack_up(g, par):
                sp.wait_ge(fq_mm, since(PAIRS * (g - 1)))
                sp.wait_ge(qk_hi_ready, 4 * (g + 1))
                for j in range(3):
                    for row in (0, 2):
                        sp.dma_start(stack[par][row * QUAD:(row + 1) * QUAD, j].bitcast(F32),
                                     qk_hi[j * QUAD:(j + 1) * QUAD].bitcast(F32)).then_inc(stacked, 16)
                sp.wait_ge(qk_lo_ready, 4 * (g + 1))
                for j in range(3):
                    sp.dma_start(stack[par][QUAD:2 * QUAD, j].bitcast(F32),
                                 qk_lo[j * QUAD:(j + 1) * QUAD].bitcast(F32)).then_inc(stacked, 16)

            load(0)
            load(1)
            load_residual(0)
            stack_up(0, 0)

            def emit(i, par, exists):
                prev2, prev, cur, nxt, nxt2 = exists
                if nxt2:
                    load(i + 2)
                if prev2:
                    sp.wait_ge(res_ready, since(G * (i - 1)))
                    sp.dma_start(mixed[bass.ds((i - 2) * G, G)].rearrange("b s d -> s b d"), h_out[:]
                                 ).then_inc(h_stored, 16)
                    if prev:
                        load_residual(i - 1)
                if nxt:
                    stack_up(i + 1, 1 - par)

            pipeline(sp, emit)
            sp.wait_ge(h_stored, 16 * GROUPS)

        @block.gpsimd
        def _(pool):
            nc.gpsimd.memset(pow_tile[:], -0.5).then_inc(const_pool, 1)
            nc.gpsimd.memset(ln_eps[:], LN_EPS).then_inc(const_pool, 1)
            nc.gpsimd.memset(eps_tile[:], KERNEL_EPS).then_inc(const_pool, 1)
            for s in range(2):
                nc.gpsimd.memset(v_aug[s][:], 1.0).then_inc(const_pool, 1)
            nc.gpsimd.memset(bounds[:], 0.0).then_inc(const_pool, 1)
            nc.gpsimd.memset(context[:], 0.0).then_inc(const_pool, 1)
            pool.wait_ge(const_pool, 7)

            def root(g):
                pool.wait_ge(moments, G * (g + 1))
                pool.wait_ge(xn_ready, since(G * g))
                nc.gpsimd.tensor_tensor(var_eps[:], bn_mv[:, :, 1], ln_eps[:], ALU.add).then_inc(var_ready, 1)
                pool.wait_ge(var_ready, g + 1)
                nc.gpsimd.tensor_tensor(rstd[:], var_eps[:], pow_tile[:], ALU.pow).then_inc(rstd_ready, 1)

            root(0)
            root(1)

            def emit(i, par, exists):
                prev2, prev, cur, nxt, nxt2 = exists
                if nxt2:
                    root(i + 2)
                if cur:
                    for b in (2, 3):
                        pool.wait_ge(kp_exp, G * i + b + 1)
                        nc.gpsimd.tensor_tensor(kp[:, b], kp[:, b],
                                                eps_tile[0:SEQ].to_broadcast([SEQ, HEADS * FEAT]),
                                                ALU.add).then_inc(kp23_ready, 1)
                    for p in range(PAIRS):
                        pool.wait_ge(qp_exp, PAIRS * i + p + 1)
                        nc.gpsimd.tensor_tensor(qp[:, p], qp[:, p], eps_tile[:].to_broadcast([P, GT]),
                                                ALU.add).then_inc(qp_ready, 1)

            pipeline(pool, emit)

        @block.scalar
        def _(act):
            def transposed_hi(g):
                act.wait_ge(v_mm, since(G * g))
                act.wait_ge(x_transposed, 2 * g + 1)
                nc.scalar.activation(xt0[:, 0], pj[1][:, 0:GT], ACT.Copy).then_inc(xt_hi, 1)
                act.wait_ge(x_transposed, 2 * g + 2)
                nc.scalar.activation(xt1[0:REST], pj[0][0:REST, 0:GT], ACT.Copy).then_inc(xt_hi, 1)

            def qk_parts(g, par, chunks):
                if chunks[0] == 0:
                    act.wait_ge(stacked, since(16 * 9 * g))
                    act.wait_ge(diag_mm, since(g - 1))
                for c in chunks:
                    act.wait_ge(qk_mm, 4 * g + c + 1)
                    nc.scalar.activation(qk_hi[:, c], pj[c % 2][0:HALF, 0:GT],
                                         ACT.Copy).then_inc(qk_hi_ready, 1)
                    nc.scalar.activation(qk_sq[par][:, c], pj[c % 2][0:HALF, 0:GT],
                                         ACT.Square).then_inc(qk_sq_ready, 1)

            def exp_k(g):
                act.wait_ge(ctx_mm, since(G * g))
                for b in range(G):
                    act.wait_ge(fk_mm, G * g + b + 1)
                    nc.scalar.activation(kp[:, b].rearrange("p (a c) -> p a c", a=2), feature_banks(b),
                                         ACT.Exp).then_inc(kp_exp, 1)

            def exp_q(g, pairs):
                act.wait_ge(att_mm, since(G * g))
                for p in pairs:
                    act.wait_ge(fq_mm, PAIRS * g + p + 1)
                    nc.scalar.activation(qp[:, p], wide[:, p % 4, 0:GT], ACT.Exp).then_inc(qp_exp, 1)

            def copy_context(g, n):
                if n == 0:
                    act.wait_ge(att_mm, since(G * g))
                act.wait_ge(ctx_mm, G * g + 2 * n + 2)
                for r in range(2):
                    rows, cols = slice(r * FEAT, (r + 1) * FEAT), slice(r * VW, (r + 1) * VW)
                    nc.scalar.activation(
                        context[rows, 2 * n:2 * n + 2, :, cols],
                        tr[n][rows, 0:2 * PAIRS * 2 * VW].rearrange(
                            "p (b q c) -> p b q c", b=2, q=PAIRS)[:, :, :, cols],
                        ACT.Copy).then_inc(ctx_ready, 1)

            def copy_values(g, par, b):
                act.wait_ge(v_mm, G * g + b + 1)
                if b == 0:
                    act.wait_ge(ctx_mm, since(G * (g - 1)))
                nc.scalar.activation(v_aug[par][:, b, :, 0:DH],
                                     pj[b % 2][0:SEQ, 0:DIM].rearrange("p (h d) -> p h d", h=HEADS),
                                     ACT.Copy).then_inc(v_ready, 1)

            def output_hi(g):
                act.wait_ge(wo_mm, since(G * g))
                act.wait_ge(o_transposed, 2 * g + 1)
                nc.scalar.activation(ot0[:, 0], pj[1][:, 0:GT], ACT.Copy).then_inc(ot_hi, 1)
                act.wait_ge(o_transposed, 2 * g + 2)
                nc.scalar.activation(ot1[0:REST], pj[0][0:REST, 0:GT], ACT.Copy).then_inc(ot_hi, 1)

            transposed_hi(0)
            qk_parts(0, 0, range(4))
            act.wait_ge(const_pool, 7)

            def emit(i, par, exists):
                prev2, prev, cur, nxt, nxt2 = exists
                if prev:
                    copy_context(i - 1, 0)
                if cur:
                    for b in range(G):
                        copy_values(i, par, b)
                if nxt:
                    transposed_hi(i + 1)
                if prev:
                    copy_context(i - 1, 1)
                if nxt:
                    qk_parts(i + 1, 1 - par, range(4))
                if cur:
                    exp_k(i)
                    exp_q(i, (0, 1))
                if prev:
                    output_hi(i - 1)
                if cur:
                    exp_q(i, (2, 3, 4, 5))

            pipeline(act, emit)

        @block.vector
        def _(dve):
            def take_moments(g):
                dve.wait_ge(h_loaded, 32 * (g + 1))
                for b in range(G):
                    nc.vector.bn_stats(bn_st[:, b], h_in[:, b]).then_inc(stats, 1)
                dve.wait_ge(stats, G * (g + 1))
                nc.vector.memset(carrier[:], 0.0)
                for b in range(G):
                    nc.vector.bn_aggr(bn_mv[:, b], bn_st[:, b]).then_inc(moments, 1)

            def norm(g):
                dve.wait_ge(rstd_ready, g + 1)
                dve.wait_ge(x_transposed, since(2 * g))
                for b in range(G):
                    nc.vector.tensor_scalar(xn[:, b], h_in[:, b], bn_mv[:, b, 0:1], rstd[:, b:b + 1],
                                            ALU.subtract, ALU.mult).then_inc(xn_ready, 1)

            def transposed_lo(g):
                dve.wait_ge(xt_hi, 2 * g + 1)
                nc.vector.tensor_tensor(xt0[:, 1], pj[1][:, 0:GT], xt0[:, 0].bitcast(F32),
                                        ALU.subtract).then_inc(xt_lo, 1)
                dve.wait_ge(xt_hi, 2 * g + 2)
                nc.vector.tensor_tensor(xt1[REST:P], pj[0][0:REST, 0:GT], xt1[0:REST].bitcast(F32),
                                        ALU.subtract).then_inc(xt_lo, 1)

            def qk_rests(g, chunks):
                for c in chunks:
                    dve.wait_ge(qk_sq_ready, 4 * g + c + 1)
                    nc.vector.tensor_tensor(qk_lo[:, c], pj[c % 2][0:HALF, 0:GT],
                                            qk_hi[:, c].bitcast(F32), ALU.subtract).then_inc(qk_lo_ready, 1)

            def maxima(g, b):
                if b == 0:
                    dve.wait_ge(bounds_tr, since(g))
                for t in range(2):
                    dve.wait_ge(dash_mm, 8 * g + 2 * b + t + 1)
                    nc.vector.tensor_reduce(
                        bounds[:, b, 2 * t * QUAD:2 * (t + 1) * QUAD].rearrange(
                            "p (a h) -> p a h", a=2)[:, :, 0:HEADS // 2],
                        wide[0:SEQ, 2 * t:2 * t + 2, 0:3 * P].rearrange("p a (h m) -> p a h m", m=FEAT),
                        AX_X, ALU.max).then_inc(maxed, 1)

            def bound_of_k(g):
                dve.wait_ge(bounds_tr, g + 1)
                dve.wait_ge(bound_k_ready, since(g))
                nc.vector.tensor_reduce(stab_k[2 * QUAD:P],
                                        wide[2 * QUAD:P, 1, 0:GT].rearrange("p (b s) -> p b s", b=G),
                                        AX_X, ALU.max).then_inc(stab_ready, 1)
                dve.wait_ge(stab_ready, g + 1)
                dve.wait_ge(nbk_ready, since(g))
                nc.vector.tensor_tensor(bound_k[:],
                                        wide[2 * QUAD:P, 0, 0:GT].rearrange("p (b s) -> p b s", b=G),
                                        stab_k[2 * QUAD:P].unsqueeze(2).to_broadcast([FEAT, G, SEQ]),
                                        ALU.add).then_inc(bound_k_ready, 1)
                flat = bound_k[:].rearrange("p b s -> p (b s)")
                dve.wait_ge(bound_k_ready, g + 1)
                dve.wait_ge(fk_mm, since(G * g))
                nc.vector.tensor_copy(nb_k[0:FEAT], flat).then_inc(nbk_hi, 1)
                dve.wait_ge(nbk_hi, g + 1)
                nc.vector.tensor_tensor(nb_k[FEAT:P], flat, nb_k[0:FEAT].bitcast(F32),
                                        ALU.subtract).then_inc(nbk_ready, 1)

            def bound_of_q(g):
                dve.wait_ge(fq_mm, since(PAIRS * g))
                nc.vector.tensor_copy(nb_q[0:FEAT], wide[0:FEAT, 0, 0:GT]).then_inc(nbq_hi, 1)
                dve.wait_ge(nbq_hi, g + 1)
                nc.vector.tensor_tensor(nb_q[FEAT:P], wide[0:FEAT, 0, 0:GT], nb_q[0:FEAT].bitcast(F32),
                                        ALU.subtract).then_inc(nbq_ready, 1)

            def add_eps(g):
                for b in range(2):
                    dve.wait_ge(kp_exp, G * g + b + 1)
                    nc.vector.tensor_scalar(kp[:, b], kp[:, b], KERNEL_EPS, None, ALU.add).then_inc(kp01_ready, 1)

            def divide(g):
                dve.wait_ge(att_mm, G * (g + 1))
                dve.wait_ge(attn_ready, since(G * g))
                sums = [tr[n][0:SEQ, 0:2 * HEADS * VW].rearrange("p (b h c) -> p b h c", b=2, h=HEADS)
                        for n in range(2)]
                for n in range(2):
                    nc.vector.reciprocal(den[:, 2 * n:2 * n + 2], sums[n][:, :, :, DH]).then_inc(den_ready, 1)
                dve.wait_ge(o_transposed, since(2 * g))
                for n in range(G):
                    dve.wait_ge(den_ready, 2 * g + 1 + n // 2)
                    nc.vector.tensor_tensor(attn[:, n].rearrange("p (h d) -> p h d", h=HEADS),
                                            sums[n // 2][:, n % 2, :, 0:DH],
                                            den[:, n].unsqueeze(2).to_broadcast([SEQ, HEADS, DH]),
                                            ALU.mult).then_inc(attn_ready, 1)

            def output_lo(g):
                dve.wait_ge(wo_mm, since(G * g))
                dve.wait_ge(ot_hi, 2 * g + 1)
                nc.vector.tensor_tensor(ot0[:, 1], pj[1][:, 0:GT], ot0[:, 0].bitcast(F32),
                                        ALU.subtract).then_inc(ot_lo, 1)
                dve.wait_ge(ot_hi, 2 * g + 2)
                nc.vector.tensor_tensor(ot1[REST:P], pj[0][0:REST, 0:GT], ot1[0:REST].bitcast(F32),
                                        ALU.subtract).then_inc(ot_lo, 1)

            def residual(g):
                dve.wait_ge(res_loaded, 32 * (g + 1))
                dve.wait_ge(h_stored, since(16 * g))
                for b in range(G):
                    dve.wait_ge(wo_mm, G * g + b + 1)
                    nc.vector.tensor_tensor(h_out[:, b], wide[0:SEQ, (b + 2) % 4, 0:DIM], h_res[:, b],
                                            ALU.add).then_inc(res_ready, 1)

            dve.wait_ge(const_pool, 7)
            take_moments(0)
            norm(0)
            transposed_lo(0)
            qk_rests(0, range(4))
            take_moments(1)

            def emit(i, par, exists):
                prev2, prev, cur, nxt, nxt2 = exists
                if nxt:
                    norm(i + 1)
                if prev2:
                    residual(i - 2)
                if cur:
                    maxima(i, 0)
                    maxima(i, 1)
                    maxima(i, 2)
                if nxt:
                    transposed_lo(i + 1)
                if cur:
                    maxima(i, 3)
                if nxt:
                    qk_rests(i + 1, (0, 1))
                if cur:
                    bound_of_k(i)
                    bound_of_q(i)
                if nxt:
                    qk_rests(i + 1, (2, 3))
                if prev:
                    divide(i - 1)
                if cur:
                    add_eps(i)
                if nxt2:
                    take_moments(i + 2)
                if prev:
                    output_lo(i - 1)

            pipeline(dve, emit)

        @block.tensor
        def _(pe):
            pe.wait_ge(const_pool, 7)

            def transpose_x(g):
                pe.wait_ge(xn_ready, G * (g + 1))
                pe.wait_ge(v_ready, since(G * g))
                for cols, out in ((slice(0, P), pj[1]), (slice(P, DIM), pj[0][0:REST])):
                    for b in range(G):
                        last = nc.tensor.transpose(out[:, tok(b)], xn[:, b, cols], w.ident[0:SEQ, 0:SEQ])
                    last.then_inc(x_transposed, 1)

            def project_qk(g, chunks):
                for c in chunks:
                    if c == 0:
                        pe.wait_ge(xt_lo, 2 * (g + 1))
                    if c >= 2:
                        pe.wait_ge(qk_lo_ready, 4 * g + c - 1)
                    ps5 = passes(c * HALF, (c + 1) * HALF, xt0, xt1, slice(0, GT))
                    for n, (wt, x) in enumerate(ps5):
                        last = nc.tensor.matmul(pj[c % 2][0:HALF, 0:GT], wt, x, start=(n == 0), stop=(n == 4))
                    last.then_inc(qk_mm, 1)

            def values(g, b):
                if b < 2:
                    pe.wait_ge(qk_lo_ready, 4 * g + b + 3)
                else:
                    pe.wait_ge(v_ready, G * g + b - 1)
                ps5 = passes(2 * DIM, 3 * DIM, xt0, xt1, tok(b))
                for n, (wt, x) in enumerate(ps5):
                    last = nc.tensor.matmul(pj[b % 2][0:SEQ, 0:DIM], x, wt, start=(n == 0), stop=(n == 4))
                last.then_inc(v_mm, 1)

            def context_of(g, par, b, pairs=range(PAIRS)):
                if b < 2:
                    pe.wait_ge(kp01_ready, 2 * g + b + 1)
                    if b == 0:
                        pe.wait_ge(attn_ready, since(G * g))
                else:
                    pe.wait_ge(kp23_ready, 2 * g + b - 1)
                for p in pairs:
                    o = (b % 2) * PAIRS * 2 * VW + p * 2 * VW
                    last = nc.tensor.matmul(
                        tr[b // 2][:, o:o + 2 * VW], kp[:, b, p * P:(p + 1) * P],
                        v_aug[par][:, b, 2 * p:2 * p + 2].rearrange("p h d -> p (h d)"), start=True, stop=True)
                if pairs[-1] == PAIRS - 1:
                    last.then_inc(ctx_mm, 1)

            def attend(g, b):
                if b == 0:
                    pe.wait_ge(qp_ready, PAIRS * (g + 1))
                if b % 2 == 0:
                    pe.wait_ge(ctx_ready, 4 * g + b + 2)
                for p in range(PAIRS):
                    o = (b % 2) * PAIRS * 2 * VW + p * 2 * VW
                    last = nc.tensor.matmul(tr[b // 2][0:SEQ, o:o + 2 * VW],
                                            qp[:, p, tok(b)], context[:, b, p], start=True, stop=True)
                last.then_inc(att_mm, 1)

            def transpose_o(g):
                pe.wait_ge(attn_ready, G * (g + 1))
                for cols, out in ((slice(0, P), pj[1]), (slice(P, DIM), pj[0][0:REST])):
                    for b in range(G):
                        last = nc.tensor.transpose(out[:, tok(b)], attn[:, b, cols], w.ident[0:SEQ, 0:SEQ])
                    last.then_inc(o_transposed, 1)

            def dash(g, par, b):
                for t in range(2):
                    if b:
                        pe.wait_ge(maxed, 8 * g + 2 * (b - 1) + t + 1)
                    for p in range(PAIRS):
                        c, j = 2 * t + p // 3, p % 3
                        last = nc.tensor.matmul(wide[0:SEQ, c, j * P:(j + 1) * P],
                                                stack[par][:, j, c, tok(b)], w.proj_st[:], start=True, stop=True)
                    last.then_inc(dash_mm, 1)

            def diag_of(g, par):
                pe.wait_ge(maxed, 8 * g + 7)
                for c in range(4):
                    last = nc.tensor.matmul(wide[c * QUAD:(c + 1) * QUAD, 0, 0:GT], w.diag_w[:], qk_sq[par][:, c],
                                            start=True, stop=(c >= 2), skip_group_check=True)
                last.then_inc(diag_mm, 1)

            def transpose_bounds(g):
                pe.wait_ge(maxed, 8 * g + 8)
                for b in range(G):
                    nc.tensor.matmul(wide[0:2 * QUAD, 0, tok(b)], bounds[:, b, 0:2 * QUAD], w.ident[0:SEQ, 0:SEQ],
                                     start=False, stop=True, skip_group_check=True)
                    last = nc.tensor.matmul(wide[2 * QUAD:P, 1, tok(b)], bounds[:, b, 2 * QUAD:P],
                                            w.ident[0:SEQ, 0:SEQ], start=True, stop=True)
                last.then_inc(bounds_tr, 1)

            def output(g, b):
                if b == 0:
                    pe.wait_ge(ot_lo, 2 * (g + 1))
                ps5 = passes(3 * DIM, 4 * DIM, ot0, ot1, tok(b))
                for n, (wt, x) in enumerate(ps5):
                    last = nc.tensor.matmul(wide[0:SEQ, (b + 2) % 4, 0:DIM], x, wt, start=(n == 0), stop=(n == 4))
                last.then_inc(wo_mm, 1)

            def features_k(g, par, nxt):
                for b in range(G):
                    if b == 0:
                        pe.wait_ge(nbk_ready, g + 1)
                    if b == 1:
                        pe.wait_ge(nbq_ready, g + 1)
                    if b == 2 and nxt:
                        pe.wait_ge(qk_lo_ready, 4 * (g + 2))
                    if b == 2 and not nxt:
                        pe.wait_ge(v_ready, G * (g + 1))
                    if b == 3:
                        pe.wait_ge(kp_exp, G * g + 1)
                    banks = feature_banks(b)
                    for a in range(2):
                        nc.tensor.matmul(banks[:, a], nb_k[:, tok(b)],
                                         w.sel[:, a * 3 * P:(a + 1) * 3 * P], start=True, stop=False,
                                         skip_group_check=True)
                        for j in range(3):
                            last = nc.tensor.matmul(banks[:, a, j * P:(j + 1) * P],
                                                    stack[par][:, j, 2 + a, tok(b)], w.proj_st[:],
                                                    start=False, stop=(j == 2), skip_group_check=True)
                    last.then_inc(fk_mm, 1)

            def features_q(g, par, pairs):
                for p in pairs:
                    if p in (0, 2):
                        pe.wait_ge(kp_exp, G * g + 2 + p)
                    if p >= 4:
                        pe.wait_ge(qp_exp, PAIRS * g + p - 3)
                    nc.tensor.matmul(wide[:, p % 4, 0:GT], w.proj_st[:], stack[par][:, p % 3, p // 3],
                                     start=True, stop=False)
                    nc.tensor.matmul(wide[:, p % 4, 0:GT], w.sel[:, p * P:(p + 1) * P], nb_q[:], start=False,
                                     stop=True).then_inc(fq_mm, 1)

            transpose_x(0)
            project_qk(0, range(4))

            def emit(i, par, exists):
                prev2, prev, cur, nxt, nxt2 = exists
                for n in range(2):
                    if prev:
                        context_of(i - 1, 1 - par, n)
                    if prev2:
                        for b in (2 * n, 2 * n + 1):
                            if prev:
                                pe.wait_ge(qp_exp, since(PAIRS * (i - 1) + b + 3))
                            output(i - 2, b)
                if cur:
                    values(i, 0)
                    values(i, 1)
                    pe.wait_ge(stacked, 16 * 9 * (i + 1))
                    if prev2:
                        pe.wait_ge(res_ready, since(G * (i - 1)))
                    elif prev:
                        pe.wait_ge(qp_exp, since(PAIRS * i))
                    dash(i, par, 0)
                if prev:
                    context_of(i - 1, 1 - par, 2)
                if cur:
                    values(i, 2)
                    dash(i, par, 1)
                if prev:
                    context_of(i - 1, 1 - par, 3, (0, 1, 2))
                    attend(i - 1, 0)
                if cur:
                    values(i, 3)
                    dash(i, par, 2)
                if prev:
                    context_of(i - 1, 1 - par, 3, (3, 4, 5))
                    attend(i - 1, 1)
                if nxt:
                    transpose_x(i + 1)
                if cur:
                    dash(i, par, 3)
                if nxt:
                    project_qk(i + 1, (0, 1))
                if cur:
                    diag_of(i, par)
                    transpose_bounds(i)
                if nxt:
                    project_qk(i + 1, (2, 3))
                if prev:
                    attend(i - 1, 2)
                    attend(i - 1, 3)
                if cur:
                    features_k(i, par, nxt)
                    features_q(i, par, (0, 1))
                if prev:
                    if cur:
                        pe.wait_ge(kp_exp, G * i + 3)
                    transpose_o(i - 1)
                if cur:
                    features_q(i, par, (2, 3, 4, 5))

            pipeline(pe, emit)


def ffn_phase(nc, w, mixed, out):
    TT = FT // P
    with ExitStack() as ctx:
        def sb(name, shape, dt=F32):
            return ctx.enter_context(nc.sbuf_tensor(name, shape, dt))

        def ps(name, shape):
            return ctx.enter_context(nc.psum_tensor(name, shape, F32))

        def sem(name):
            return ctx.enter_context(nc.semaphore(name))

        pow_tile = sb("f_pow", [P, TT])
        ln_eps = sb("f_ln_eps", [P, TT])
        h_in = [sb(f"f_h_in{s}", [P, TT, DIM]) for s in range(2)]
        bn_st = sb("f_bn_st", [P, TT, 6])
        bn_mv = [sb(f"f_bn_mv{s}", [P, TT, 2]) for s in range(2)]
        var_eps = sb("f_var_eps", [P, TT])
        rstd = sb("f_rstd", [P, TT])
        carrier = sb("f_carrier", [1, 1])
        xn = sb("f_xn", [P, TT, DIM])
        xt0 = [sb(f"f_xt0_{s}", [P, 2, FT], F32R) for s in range(2)]
        xt1 = [sb(f"f_xt1_{s}", [P, FT], F32R) for s in range(2)]
        hid = sb("f_hid", [P, HC, FT])
        hid_hi = sb("f_hid_hi", [P, HC, FT], F32R)
        hid_lo = sb("f_hid_lo", [P, HC, FT], F32R)
        h_res = sb("f_h_res", [P, TT, DIM])
        part = sb("f_part", [P, TT, DIM])
        h_out = sb("f_h_out", [P, TT, DIM])

        tr = [ps("f_tr0", [P, 512]), ps("f_tr1", [P, 512])]
        up = [ps("f_up0", [P, 512]), ps("f_up1", [P, 512])]
        down = [[ps(f"f_down{s}{b}", [P, 512]) for b in range(TT)] for s in range(2)]

        const_pool = sem("f_const_pool")
        h_loaded = sem("f_h_loaded")
        stats = sem("f_stats")
        moments = sem("f_moments")
        var_ready = sem("f_var_ready")
        rstd_ready = sem("f_rstd_ready")
        xn_ready = sem("f_xn_ready")
        x_transposed = sem("f_x_transposed")
        xt_hi = sem("f_xt_hi")
        xt_lo = sem("f_xt_lo")
        up_mm = sem("f_up_mm")
        gelu_done = sem("f_gelu_done")
        hid_hi_ready = sem("f_hid_hi_ready")
        hid_lo_ready = sem("f_hid_lo_ready")
        down_mm = sem("f_down_mm")
        res_loaded = sem("f_res_loaded")
        part_ready = sem("f_part_ready")
        res_ready = sem("f_res_ready")
        stored = sem("f_stored")
        block = ctx.enter_context(nc.Block())

        rows_in = mixed.flatten_outer_dims()
        rows_out = out.flatten_outer_dims()

        def tile_rows(rows, g):
            return rows[bass.ds(g * FT, FT), :].rearrange("(a p) d -> p a d", p=P)

        LOOP_FROM, LOOP_TO = 3, F_ITERS - 2

        def pipeline(eng, emit):
            def single(i):
                emit(i, i % 2, [0 <= i + d < F_ITERS for d in (-2, -1, 0, 1, 2)])

            for i in range(LOOP_FROM):
                single(i)
            with eng.Fori(LOOP_FROM, LOOP_TO - 1, 2) as i:
                emit(i, LOOP_FROM % 2, [True] * 5)
                emit(i + 1, (LOOP_FROM + 1) % 2, [True] * 5)
            for i in range(LOOP_TO, F_ITERS + 2):
                single(i)

        @block.sync
        def _(sp):
            def load(g, par):
                sp.wait_ge(xn_ready, since(TT * g))
                sp.dma_start(h_in[par][:], tile_rows(rows_in, g)).then_inc(h_loaded, 16)

            def load_residual(g):
                sp.wait_ge(part_ready, since(TT * g))
                sp.dma_start(h_res[:], tile_rows(rows_in, g)).then_inc(res_loaded, 16)

            load(0, 0)
            load(1, 1)
            load_residual(0)

            def emit(i, par, exists):
                prev2, prev, cur, nxt, nxt2 = exists
                if nxt2:
                    load(i + 2, par)
                if prev2:
                    if prev:
                        load_residual(i - 1)
                    sp.wait_ge(res_ready, since(TT * (i - 1)))
                    sp.dma_start(tile_rows(rows_out, i - 2), h_out[:]).then_inc(stored, 16)

            pipeline(sp, emit)
            sp.wait_ge(stored, 16 * F_ITERS)

        @block.gpsimd
        def _(pool):
            nc.gpsimd.memset(pow_tile[:], -0.5).then_inc(const_pool, 1)
            nc.gpsimd.memset(ln_eps[:], LN_EPS).then_inc(const_pool, 1)
            pool.wait_ge(const_pool, 2)

            def root(g, par):
                pool.wait_ge(moments, TT * (g + 1))
                pool.wait_ge(xn_ready, since(TT * g))
                nc.gpsimd.tensor_tensor(var_eps[:], bn_mv[par][:, :, 1], ln_eps[:], ALU.add).then_inc(var_ready, 1)
                pool.wait_ge(var_ready, g + 1)
                nc.gpsimd.tensor_tensor(rstd[:], var_eps[:], pow_tile[:], ALU.pow).then_inc(rstd_ready, 1)

            root(0, 0)
            root(1, 1)

            def emit(i, par, exists):
                prev2, prev, cur, nxt, nxt2 = exists
                if nxt2:
                    root(i + 2, par)

            pipeline(pool, emit)

        @block.scalar
        def _(act):
            def transposed_hi(g, par):
                act.wait_ge(up_mm, since(HC * (g - 1)))
                act.wait_ge(x_transposed, 2 * g + 1)
                nc.scalar.activation(xt0[par][:, 0], tr[0][:, 0:FT], ACT.Copy).then_inc(xt_hi, 1)
                act.wait_ge(x_transposed, 2 * g + 2)
                nc.scalar.activation(xt1[par][0:REST], tr[1][0:REST, 0:FT], ACT.Copy).then_inc(xt_hi, 1)

            transposed_hi(0, 0)

            def emit(i, par, exists):
                prev2, prev, cur, nxt, nxt2 = exists
                if not cur:
                    return
                for c in range(HC):
                    act.wait_ge(up_mm, HC * i + c + 1)
                    act.wait_ge(hid_lo_ready, since(HC * (i - 1) + c + 1 if prev else 0))
                    nc.scalar.activation(hid[:, c], up[c % 2][:, 0:FT], ACT.Gelu,
                                         bias=w.b1[:, c:c + 1]).then_inc(gelu_done, 1)
                    act.wait_ge(down_mm, since(HC * (i - 1) + c + 1 if prev else 0))
                    nc.scalar.activation(hid_hi[:, c], up[c % 2][:, 0:FT], ACT.Gelu,
                                         bias=w.b1[:, c:c + 1]).then_inc(hid_hi_ready, 1)
                    if c == 2 and nxt:
                        transposed_hi(i + 1, 1 - par)

            pipeline(act, emit)

        @block.vector
        def _(dve):
            def take_moments(g, par):
                dve.wait_ge(h_loaded, 16 * (g + 1))
                for b in range(TT):
                    nc.vector.bn_stats(bn_st[:, b], h_in[par][:, b]).then_inc(stats, 1)
                dve.wait_ge(stats, TT * (g + 1))
                nc.vector.memset(carrier[:], 0.0)
                for b in range(TT):
                    nc.vector.bn_aggr(bn_mv[par][:, b], bn_st[:, b]).then_inc(moments, 1)

            def norm(g, par):
                dve.wait_ge(rstd_ready, g + 1)
                dve.wait_ge(x_transposed, since(2 * g))
                for b in range(TT):
                    nc.vector.tensor_scalar(xn[:, b], h_in[par][:, b], bn_mv[par][:, b, 0:1], rstd[:, b:b + 1],
                                            ALU.subtract, ALU.mult).then_inc(xn_ready, 1)

            def transposed_lo(g, par):
                dve.wait_ge(xt_hi, 2 * g + 1)
                nc.vector.tensor_tensor(xt0[par][:, 1], tr[0][:, 0:FT], xt0[par][:, 0].bitcast(F32),
                                        ALU.subtract).then_inc(xt_lo, 1)
                dve.wait_ge(xt_hi, 2 * g + 2)
                nc.vector.tensor_tensor(xt1[par][REST:P], tr[1][0:REST, 0:FT], xt1[par][0:REST].bitcast(F32),
                                        ALU.subtract).then_inc(xt_lo, 1)

            def residual(g, par):
                dve.wait_ge(res_loaded, 16 * (g + 1))
                dve.wait_ge(res_ready, since(TT * g))
                dve.wait_ge(down_mm, HC * (g + 1))
                for b in range(TT):
                    nc.vector.tensor_tensor(part[:, b], down[par][b][:, DIM:2 * DIM], h_res[:, b],
                                            ALU.add).then_inc(part_ready, 1)
                dve.wait_ge(part_ready, TT * (g + 1))
                dve.wait_ge(stored, since(16 * g))
                for b in range(TT):
                    nc.vector.tensor_tensor(h_out[:, b], down[par][b][:, 0:DIM], part[:, b],
                                            ALU.add).then_inc(res_ready, 1)

            take_moments(0, 0)
            norm(0, 0)
            take_moments(1, 1)
            transposed_lo(0, 0)

            def emit(i, par, exists):
                prev2, prev, cur, nxt, nxt2 = exists
                if nxt:
                    norm(i + 1, 1 - par)
                if prev2:
                    residual(i - 2, par)
                if cur:
                    for c in range(HC):
                        dve.wait_ge(hid_hi_ready, HC * i + c + 1)
                        dve.wait_ge(down_mm, since(HC * (i - 1) + c + 1 if prev else 0))
                        nc.vector.tensor_tensor(hid_lo[:, c], hid[:, c], hid_hi[:, c].bitcast(F32),
                                                ALU.subtract).then_inc(hid_lo_ready, 1)
                        if c == 2 and nxt:
                            transposed_lo(i + 1, 1 - par)
                        if c == 3 and nxt2:
                            take_moments(i + 2, par)

            pipeline(dve, emit)

        @block.tensor
        def _(pe):
            def transpose_x(g):
                pe.wait_ge(xn_ready, TT * (g + 1))
                pe.wait_ge(xt_lo, since(2 * g))
                for cols, bank in ((slice(0, P), tr[0]), (slice(P, DIM), tr[1][0:REST])):
                    for b in range(TT):
                        last = nc.tensor.transpose(bank[:, b * P:(b + 1) * P], xn[:, b, cols], w.ident[:])
                    last.then_inc(x_transposed, 1)

            def up_chunk(g, par, c):
                if c == 0:
                    pe.wait_ge(xt_lo, 2 * (g + 1))
                pe.wait_ge(gelu_done, since(HC * g + c - 1))
                pe.wait_ge(hid_hi_ready, since(HC * g + c - 1))
                s = slice(c * P, (c + 1) * P)
                ps5 = split_passes(w.w1a_hi[:, s], w.w1a_lo[:, s], w.w1b_hi[:, s], w.w1b_lo[0:REST, s],
                                   xt0[par][:, 0], xt0[par][:, 1], xt1[par][:])
                for n, (wt, x) in enumerate(ps5):
                    last = nc.tensor.matmul(up[c % 2][:, 0:FT], wt, x, start=(n == 0), stop=(n == 4))
                last.then_inc(up_mm, 1)

            def down_chunk(g, par, c):
                if c == 0:
                    pe.wait_ge(res_ready, since(TT * (g - 1)))
                pe.wait_ge(hid_lo_ready, HC * g + c + 1)
                for b in range(TT):
                    t = slice(b * P, (b + 1) * P)
                    nc.tensor.matmul(down[par][b][:, 0:2 * DIM], hid_hi[:, c, t],
                                     w.w2_parts[:, c].rearrange("p k n -> p (k n)"),
                                     start=(c == 0), stop=False, skip_group_check=True)
                    last = nc.tensor.matmul(down[par][b][:, 0:DIM], hid_lo[:, c, t], w.w2_parts[:, c, 0],
                                            start=False, stop=(c == HC - 1), skip_group_check=True)
                last.then_inc(down_mm, 1)

            transpose_x(0)

            def emit(i, par, exists):
                prev2, prev, cur, nxt, nxt2 = exists
                for c in range(HC):
                    if cur:
                        up_chunk(i, par, c)
                    if prev:
                        down_chunk(i - 1, 1 - par, c)
                    if c == 2 and nxt:
                        transpose_x(i + 1)

            pipeline(pe, emit)


def build_program(nc, x_tiles, txt, tok_w, tok_b, w_all, proj_t, w1_t, b1, w2, out):
    patches = nc.dram_tensor("patches", (IMAGES * PATCHES, DIM), F32, kind="Internal").ap()
    mixed = nc.dram_tensor("mixed", (IMAGES, SEQ, DIM), F32, kind="Internal").ap()
    with ExitStack() as ctx:
        w = Weights(nc, ctx)
        embed_phase(nc, w, x_tiles, tok_w, tok_b, w_all, proj_t, w1_t, b1, w2, patches)
        attention_phase(nc, w, patches, txt, mixed)
        ffn_phase(nc, w, mixed, out)


def kernel(**inputs):
    import concourse.bacc as bacc
    from concourse.bass_utils import run_bass_kernel_spmd

    a = {k: np.asarray(v) for k, v in inputs.items()}
    x = a["x"].reshape(IMAGES, GRID, PATCH, GRID, PATCH, CHANNELS).transpose(2, 4, 5, 0, 1, 3)
    x = x.reshape(KC, P, EMB_TILES // SUB, SUB * P).transpose(2, 1, 0, 3)
    layout = {
        "x_tiles": x,
        "txt_in": a["txt"],
        "tok_w": a["L0_tok_W"],
        "tok_b": a["L0_tok_b"],
        "w_all": np.concatenate([a["L0_attn_Wq"], a["L0_attn_Wk"], a["L0_attn_Wv"], a["L0_attn_Wo"]], axis=1),
        "proj_t": a["L0_attn_proj"].T,
        "w1_t": a["L0_ffn_in_weight"].T,
        "b1": a["L0_ffn_in_bias"].reshape(HC, P).T,
        "w2": a["L0_ffn_out_weight"],
    }
    nc = bacc.Bacc("TRN2", target_bir_lowering=False, num_devices=1)
    arrays, args = {}, []
    for name, value in layout.items():
        arrays[name] = np.ascontiguousarray(value)
        args.append(nc.dram_tensor(name, arrays[name].shape, F32, kind="ExternalInput").ap())
    out = nc.dram_tensor("out", (IMAGES, SEQ, DIM), F32, kind="ExternalOutput").ap()
    build_program(nc, *args, out)
    result = run_bass_kernel_spmd(nc, [arrays], core_ids=[0])
    return result.results[0]["out"]
```

```python
from contextlib import ExitStack

import numpy as np

import concourse.bass as bass
from concourse import mybir
from concourse.alu_op_type import AluOpType as ALU

F32 = mybir.dt.float32
F32R = mybir.dt.float32r
ACT = mybir.ActivationFunctionType
AX_X = mybir.AxisListType.X
P = 128

IMAGES, SIDE, CHANNELS, PATCH = 64, 96, 3, 16
GRID = SIDE // PATCH
PATCHES = GRID * GRID
TEXT = 32
SEQ = PATCHES + TEXT
DIM, HEADS = 192, 12
DH = DIM // HEADS
FEAT = 64
PATCH_DIM = PATCH * PATCH * CHANNELS
KC = PATCH_DIM // P
HID = 768
HC = HID // P
LN_EPS = 1e-5
KERNEL_EPS = 1e-4
REST = DIM - P
PAIRS = HEADS // 2
HALF = DIM // 2
VW = DH + 1
QUAD = 32

G = 4
GROUPS = IMAGES // G
GT = G * SEQ

EMB_TILES = IMAGES * PATCHES // P
SUB = 2
LOADS = 3
BODY = SUB * LOADS
ROUNDS = EMB_TILES // BODY
RING = 3

FT = 256
F_ITERS = IMAGES * SEQ // FT
TT = FT // P


def split_passes(hi0, lo0, hi1, lo1, x_hi0, x_lo0, x_st1):
    return [(hi0, x_hi0), (lo0, x_hi0), (hi0, x_lo0), (hi1, x_st1), (lo1, x_st1[0:REST])]


def since(value):
    return max(value, 0) if isinstance(value, int) else value


class Weights:

    def __init__(self, nc, ctx):
        def sb(name, shape, dt=F32):
            return ctx.enter_context(nc.sbuf_tensor(name, shape, dt))

        self.w0_hi = sb("w0_hi", [P, 4 * DIM], F32R)
        self.w0_lo = sb("w0_lo", [P, 4 * DIM], F32R)
        self.w1_hi = sb("w1_hi", [P, 4 * DIM], F32R)
        self.w1_lo = sb("w1_lo", [P, 4 * DIM], F32R)
        self.proj_st = sb("proj_st", [P, P], F32R)
        self.sel = sb("sel", [P, HEADS * FEAT], F32R)
        self.diag_w = sb("diag_w", [HALF, QUAD])
        self.ident = sb("ident", [P, P])
        self.w1a_hi = sb("w1a_hi", [P, HID], F32R)
        self.w1a_lo = sb("w1a_lo", [P, HID], F32R)
        self.w1b_hi = sb("w1b_hi", [P, HID], F32R)
        self.w1b_lo = sb("w1b_lo", [P, HID], F32R)
        self.w2_parts = sb("w2_parts", [P, HC, 2, DIM], F32R)
        self.b1 = sb("b1_sb", [P, HC])


class Embedding:

    def __init__(self, nc, ctx, raw, acc, x_tiles, tok_w, tok_b, patches):
        def sb(name, shape, dt=F32):
            return ctx.enter_context(nc.sbuf_tensor(name, shape, dt))

        def sem(name):
            return ctx.enter_context(nc.semaphore(name))

        self.nc, self.raw, self.acc = nc, raw, acc
        self.x_tiles, self.tok_w, self.tok_b, self.patches = x_tiles, tok_w, tok_b, patches
        self.w_raw = sb("emb_w_raw", [P, KC, DIM])
        self.w_parts = sb("emb_w_parts", [P, KC, 2, DIM], F32R)
        self.bias = sb("emb_bias", [P, DIM])
        self.x_hi = sb("emb_x_hi", [P, RING, KC, P], F32R)
        self.x_lo = sb("emb_x_lo", [P, RING, KC, P], F32R)
        self.part = sb("emb_part", [P, RING, DIM])
        self.emb = sb("emb_out", [P, RING, DIM])
        self.tok_w_in = sem("emb_tok_w_in")
        self.tok_b_in = sem("emb_tok_b_in")
        self.first_loaded = sem("emb_first_loaded")
        self.loaded = [sem(f"emb_loaded{s}") for s in range(LOADS)]
        self.w_split = sem("emb_w_split")
        self.hi_done = sem("emb_hi_done")
        self.lo_done = sem("emb_lo_done")
        self.mm_done = sem("emb_mm_done")
        self.part_done = sem("emb_part_done")
        self.out_done = sem("emb_out_done")
        self.stored = [sem(f"emb_stored{s}") for s in range(RING)]


    def sync_first(self, sp):
        def load(n):
            sp.dma_start(self.raw[n], self.x_tiles[n]).then_inc(self.loaded[n], 16)

        sp.dma_start(self.w_raw[:], self.tok_w.rearrange("(c p) n -> p c n", p=P)).then_inc(self.tok_w_in, 16)
        sp.dma_start(self.raw[0][:, :, 0:P], self.x_tiles[0][:, :, 0:P]).then_inc(self.first_loaded, 16)
        sp.dma_start(self.raw[0][:, :, P:SUB * P], self.x_tiles[0][:, :, P:SUB * P]).then_inc(self.loaded[0], 16)
        sp.dma_start(self.bias[:], self.tok_b.unsqueeze(0).to_broadcast([P, DIM])).then_inc(self.tok_b_in, 16)
        for n in range(1, LOADS):
            load(n)

    def sync_tile(self, sp, r, u, more=True):
        t = r * BODY + u
        if u % SUB == 0 and more:
            k = u // SUB
            sp.wait_ge(self.lo_done, t + SUB)
            sp.dma_start(self.raw[k], self.x_tiles[bass.ds(r * LOADS + (k + LOADS), 1)].squeeze(0)
                         ).then_inc(self.loaded[k], 16)
        sp.wait_ge(self.out_done, t + 1)
        sp.dma_start(self.patches[bass.ds(t * P, P), :], self.emb[:, u % RING]).then_inc(self.stored[u % RING], 16)

    def scalar_tile(self, act, r, u):
        t = r * BODY + u
        n, s = u // SUB, u % SUB
        if isinstance(r, int) and t == 0:
            act.wait_ge(self.first_loaded, 16)
        elif s == 0 or (isinstance(r, int) and t == 1):
            act.wait_ge(self.loaded[n], 16 * (r + 1))
        act.wait_ge(self.mm_done, since(t - RING + 1))
        self.nc.scalar.activation(self.x_hi[:, u % RING], self.raw[n][:, :, s * P:(s + 1) * P],
                                  ACT.Copy).then_inc(self.hi_done, 1)

    def vector_first(self, dve):
        dve.wait_ge(self.tok_w_in, 16)
        self.nc.vector.tensor_copy(self.w_parts[:, :, 0], self.w_raw[:]).then_inc(self.w_split, 1)
        dve.wait_ge(self.w_split, 1)
        self.nc.vector.tensor_tensor(self.w_parts[:, :, 1], self.w_raw[:], self.w_parts[:, :, 0].bitcast(F32),
                                     ALU.subtract).then_inc(self.w_split, 1)

    def vector_finish(self, dve, r, u):
        t, s = r * BODY + u, u % RING
        if isinstance(r, int) and t == 0:
            dve.wait_ge(self.tok_b_in, 16)
        dve.wait_ge(self.mm_done, t + 1)
        dve.wait_ge(self.out_done, since(t - RING + 1))
        self.nc.vector.tensor_tensor(self.part[:, s], self.acc[s][:, DIM:2 * DIM], self.bias[:],
                                     ALU.add).then_inc(self.part_done, 1)
        dve.wait_ge(self.part_done, t + 1)
        dve.wait_ge(self.stored[s], 16 * (r * (BODY // RING) + u // RING))
        self.nc.vector.tensor_tensor(self.emb[:, s], self.acc[s][:, 0:DIM], self.part[:, s],
                                     ALU.add).then_inc(self.out_done, 1)

    def vector_tile(self, dve, r, u):
        t = r * BODY + u
        n, s = u // SUB, u % SUB
        dve.wait_ge(self.hi_done, t + 1)
        dve.wait_ge(self.mm_done, since(t - RING + 1))
        self.nc.vector.tensor_tensor(self.x_lo[:, u % RING], self.raw[n][:, :, s * P:(s + 1) * P],
                                     self.x_hi[:, u % RING].bitcast(F32), ALU.subtract).then_inc(self.lo_done, 1)
        if u >= 2:
            self.vector_finish(dve, r, u - 2)
        elif not isinstance(r, int) or r > 0:
            self.vector_finish(dve, r - 1, BODY - 2 + u)

    def tensor_tile(self, pe, r, u):
        t, s = r * BODY + u, u % RING
        pe.wait_ge(self.lo_done, t + 1)
        pe.wait_ge(self.out_done, since(t - RING + 1))
        for c in range(KC):
            self.nc.tensor.matmul(self.acc[s][:, 0:2 * DIM], self.x_hi[:, s, c],
                                  self.w_parts[:, c].rearrange("p k n -> p (k n)"),
                                  start=(c == 0), stop=False, skip_group_check=True)
            last = self.nc.tensor.matmul(self.acc[s][:, 0:DIM], self.x_lo[:, s, c], self.w_parts[:, c, 0],
                                         start=False, stop=(c == KC - 1), skip_group_check=True)
        last.then_inc(self.mm_done, 1)

    def rounds(self, eng, tile, between=lambda: None):
        for u in range(BODY):
            tile(eng, 0, u)
        between()
        with eng.Fori(1, ROUNDS - 1) as r:
            for u in range(BODY):
                tile(eng, r, u)


class FeedForward:

    def __init__(self, nc, ctx, w, e, banks, mixed, mixed_stored, out):
        def sb(name, shape, dt=F32):
            return ctx.enter_context(nc.sbuf_tensor(name, shape, dt))

        def sem(name):
            return ctx.enter_context(nc.semaphore(name))

        def cut(buffer, *sizes):
            letters = " ".join("abcd"[:len(buffer.shape) - 1])
            flat = buffer.rearrange(f"p {letters} -> p ({letters})")
            ends = np.cumsum(sizes)
            return [flat[:, int(end - size):int(end)] for size, end in zip(sizes, ends)]

        def rows(piece):
            return piece.rearrange("p (b d) -> p b d", b=TT)

        self.nc, self.w, self.mixed_stored = nc, w, mixed_stored
        row, wide_row = TT * DIM, HC * FT
        h_in0, h_in1, xn = cut(e.raw[0], row, row, row)
        h_res, part, h_out = cut(e.raw[1], row, row, row)
        hid, = cut(e.raw[2], wide_row)
        hid_hi, = cut(e.x_hi[:], wide_row)
        hid_lo, = cut(e.x_lo[:], wide_row)
        xt00, xt01, xt10, xt11 = cut(e.w_parts[:], 2 * FT, 2 * FT, FT, FT)
        self.h_in = [rows(h_in0), rows(h_in1)]
        self.xn = rows(xn)
        self.xt0 = [x.rearrange("p (k t) -> p k t", k=2) for x in (xt00, xt01)]
        self.xt1 = [xt10, xt11]
        self.hid, self.hid_hi, self.hid_lo = (x.rearrange("p (c t) -> p c t", c=HC) for x in (hid, hid_hi, hid_lo))
        self.h_res, self.part, self.h_out = rows(h_res), rows(part), rows(h_out)
        self.pow_tile = sb("f_pow", [P, TT])
        self.ln_eps = sb("f_ln_eps", [P, TT])
        self.bn_st = sb("f_bn_st", [P, TT, 6])
        self.bn_mv = [sb(f"f_bn_mv{s}", [P, TT, 2]) for s in range(2)]
        self.var_eps = sb("f_var_eps", [P, TT])
        self.rstd = sb("f_rstd", [P, TT])
        self.carrier = sb("f_carrier", [1, 1])
        self.tr, self.up, self.down = banks

        self.const_pool = sem("f_const_pool")
        self.h_loaded = sem("f_h_loaded")
        self.stats = sem("f_stats")
        self.moments = sem("f_moments")
        self.var_ready = sem("f_var_ready")
        self.rstd_ready = sem("f_rstd_ready")
        self.xn_ready = sem("f_xn_ready")
        self.x_transposed = sem("f_x_transposed")
        self.xt_hi = sem("f_xt_hi")
        self.xt_lo = sem("f_xt_lo")
        self.up_mm = sem("f_up_mm")
        self.gelu_done = sem("f_gelu_done")
        self.hid_hi_ready = sem("f_hid_hi_ready")
        self.hid_lo_ready = sem("f_hid_lo_ready")
        self.down_mm = sem("f_down_mm")
        self.res_loaded = sem("f_res_loaded")
        self.part_ready = sem("f_part_ready")
        self.res_ready = sem("f_res_ready")
        self.stored = sem("f_stored")
        self.rows_in = mixed.flatten_outer_dims()
        self.rows_out = out.flatten_outer_dims()

    def rows(self, dram, g):
        return dram[bass.ds(g * FT, FT), :].rearrange("(a p) d -> p a d", p=P)

    def pipeline(self, eng, cycle):
        def single(i):
            cycle(eng, i, i % 2, [0 <= i + d < F_ITERS for d in (-2, -1, 0, 1, 2)])

        single(2)
        with eng.Fori(3, F_ITERS - 3, 2) as i:
            cycle(eng, i, 1, [True] * 5)
            cycle(eng, i + 1, 0, [True] * 5)
        for i in range(F_ITERS - 2, F_ITERS + 2):
            single(i)

    def load(self, sp, g, par):
        if isinstance(g, int) and g < GROUPS:
            sp.wait_ge(self.mixed_stored, 16 * (g + 1))
        sp.wait_ge(self.xn_ready, since(TT * g))
        sp.dma_start(self.h_in[par][:], self.rows(self.rows_in, g)).then_inc(self.h_loaded, 16)

    def load_residual(self, sp, g):
        sp.wait_ge(self.part_ready, since(TT * g))
        sp.dma_start(self.h_res[:], self.rows(self.rows_in, g)).then_inc(self.res_loaded, 16)

    def root(self, pool, g, par):
        pool.wait_ge(self.moments, TT * (g + 1))
        pool.wait_ge(self.xn_ready, since(TT * g))
        self.nc.gpsimd.tensor_tensor(self.var_eps[:], self.bn_mv[par][:, :, 1], self.ln_eps[:],
                                     ALU.add).then_inc(self.var_ready, 1)
        pool.wait_ge(self.var_ready, g + 1)
        self.nc.gpsimd.tensor_tensor(self.rstd[:], self.var_eps[:], self.pow_tile[:], ALU.pow).then_inc(self.rstd_ready, 1)

    def transposed_hi(self, act, g, par):
        act.wait_ge(self.up_mm, since(HC * (g - 1)))
        act.wait_ge(self.x_transposed, 2 * g + 1)
        self.nc.scalar.activation(self.xt0[par][:, 0], self.tr[0][:, 0:FT], ACT.Copy).then_inc(self.xt_hi, 1)
        act.wait_ge(self.x_transposed, 2 * g + 2)
        self.nc.scalar.activation(self.xt1[par][0:REST], self.tr[1][0:REST, 0:FT], ACT.Copy).then_inc(self.xt_hi, 1)

    def take_moments(self, dve, g, par):
        dve.wait_ge(self.h_loaded, 16 * (g + 1))
        for b in range(TT):
            self.nc.vector.bn_stats(self.bn_st[:, b], self.h_in[par][:, b]).then_inc(self.stats, 1)
        dve.wait_ge(self.stats, TT * (g + 1))
        self.nc.vector.memset(self.carrier[:], 0.0)
        for b in range(TT):
            self.nc.vector.bn_aggr(self.bn_mv[par][:, b], self.bn_st[:, b]).then_inc(self.moments, 1)

    def norm(self, dve, g, par):
        dve.wait_ge(self.rstd_ready, g + 1)
        dve.wait_ge(self.x_transposed, since(2 * g))
        for b in range(TT):
            self.nc.vector.tensor_scalar(self.xn[:, b], self.h_in[par][:, b], self.bn_mv[par][:, b, 0:1],
                                         self.rstd[:, b:b + 1], ALU.subtract, ALU.mult).then_inc(self.xn_ready, 1)

    def transposed_lo(self, dve, g, par):
        dve.wait_ge(self.xt_hi, 2 * g + 1)
        self.nc.vector.tensor_tensor(self.xt0[par][:, 1], self.tr[0][:, 0:FT], self.xt0[par][:, 0].bitcast(F32),
                                ALU.subtract).then_inc(self.xt_lo, 1)
        dve.wait_ge(self.xt_hi, 2 * g + 2)
        self.nc.vector.tensor_tensor(self.xt1[par][REST:P], self.tr[1][0:REST, 0:FT], self.xt1[par][0:REST].bitcast(F32),
                                ALU.subtract).then_inc(self.xt_lo, 1)

    def residual(self, dve, g, par):
        dve.wait_ge(self.res_loaded, 16 * (g + 1))
        dve.wait_ge(self.res_ready, since(TT * g))
        dve.wait_ge(self.down_mm, HC * (g + 1))
        for b in range(TT):
            self.nc.vector.tensor_tensor(self.part[:, b], self.down[par][b][:, DIM:2 * DIM], self.h_res[:, b],
                                    ALU.add).then_inc(self.part_ready, 1)
        dve.wait_ge(self.part_ready, TT * (g + 1))
        dve.wait_ge(self.stored, since(16 * g))
        for b in range(TT):
            self.nc.vector.tensor_tensor(self.h_out[:, b], self.down[par][b][:, 0:DIM], self.part[:, b],
                                    ALU.add).then_inc(self.res_ready, 1)

    def transpose_x(self, pe, g):
        pe.wait_ge(self.xn_ready, TT * (g + 1))
        pe.wait_ge(self.xt_lo, since(2 * g))
        for cols, bank in ((slice(0, P), self.tr[0]), (slice(P, DIM), self.tr[1][0:REST])):
            for b in range(TT):
                last = self.nc.tensor.transpose(bank[:, b * P:(b + 1) * P], self.xn[:, b, cols], self.w.ident[:])
            last.then_inc(self.x_transposed, 1)

    def up_chunk(self, pe, g, par, c):
        if c == 0:
            pe.wait_ge(self.xt_lo, 2 * (g + 1))
        pe.wait_ge(self.gelu_done, since(HC * g + c - 1))
        pe.wait_ge(self.hid_hi_ready, since(HC * g + c - 1))
        s = slice(c * P, (c + 1) * P)
        ps5 = split_passes(self.w.w1a_hi[:, s], self.w.w1a_lo[:, s], self.w.w1b_hi[:, s], self.w.w1b_lo[0:REST, s],
                           self.xt0[par][:, 0], self.xt0[par][:, 1], self.xt1[par][:])
        for n, (wt, x) in enumerate(ps5):
            last = self.nc.tensor.matmul(self.up[c % 2][:, 0:FT], wt, x, start=(n == 0), stop=(n == 4))
        last.then_inc(self.up_mm, 1)

    def down_chunk(self, pe, g, par, c):
        if c == 0:
            pe.wait_ge(self.res_ready, since(TT * (g - 1)))
        pe.wait_ge(self.hid_lo_ready, HC * g + c + 1)
        for b in range(TT):
            t = slice(b * P, (b + 1) * P)
            self.nc.tensor.matmul(self.down[par][b][:, 0:2 * DIM], self.hid_hi[:, c, t],
                             self.w.w2_parts[:, c].rearrange("p k n -> p (k n)"),
                             start=(c == 0), stop=False, skip_group_check=True)
            last = self.nc.tensor.matmul(self.down[par][b][:, 0:DIM], self.hid_lo[:, c, t], self.w.w2_parts[:, c, 0],
                                    start=False, stop=(c == HC - 1), skip_group_check=True)
        last.then_inc(self.down_mm, 1)

    def gelu(self, act, g, c, prev):
        bank = self.up[c % 2][:, 0:FT]
        act.wait_ge(self.up_mm, HC * g + c + 1)
        if prev:
            act.wait_ge(self.hid_lo_ready, HC * (g - 1) + c + 1)
        self.nc.scalar.activation(self.hid[:, c], bank, ACT.Gelu, bias=self.w.b1[:, c:c + 1]
                                  ).then_inc(self.gelu_done, 1)
        if prev:
            act.wait_ge(self.down_mm, HC * (g - 1) + c + 1)
        self.nc.scalar.activation(self.hid_hi[:, c], bank, ACT.Gelu, bias=self.w.b1[:, c:c + 1]
                                  ).then_inc(self.hid_hi_ready, 1)

    def hidden_lo(self, dve, g, c, prev):
        dve.wait_ge(self.hid_hi_ready, HC * g + c + 1)
        if prev:
            dve.wait_ge(self.down_mm, HC * (g - 1) + c + 1)
        self.nc.vector.tensor_tensor(self.hid_lo[:, c], self.hid[:, c], self.hid_hi[:, c].bitcast(F32),
                                     ALU.subtract).then_inc(self.hid_lo_ready, 1)


    def sync_cycle(self, sp, i, par, exists):
        prev2, prev, cur, nxt, nxt2 = exists
        if nxt2:
            self.load(sp, i + 2, par)
        if prev:
            self.load_residual(sp, i - 1)
        if prev2:
            sp.wait_ge(self.res_ready, TT * (i - 1))
            sp.dma_start(self.rows(self.rows_out, i - 2), self.h_out[:]).then_inc(self.stored, 16)

    def gpsimd_cycle(self, pool, i, par, exists):
        prev2, prev, cur, nxt, nxt2 = exists
        if nxt2:
            self.root(pool, i + 2, par)

    def scalar_cycle(self, act, i, par, exists):
        prev2, prev, cur, nxt, nxt2 = exists
        if cur:
            for c in range(HC):
                self.gelu(act, i, c, prev)
                if c == 2 and nxt:
                    self.transposed_hi(act, i + 1, 1 - par)

    def vector_cycle(self, dve, i, par, exists):
        prev2, prev, cur, nxt, nxt2 = exists
        if nxt:
            self.norm(dve, i + 1, 1 - par)
        if prev2:
            self.residual(dve, i - 2, par)
        if cur:
            for c in range(HC):
                self.hidden_lo(dve, i, c, prev)
                if c == 2 and nxt:
                    self.transposed_lo(dve, i + 1, 1 - par)
                if c == 3 and nxt2:
                    self.take_moments(dve, i + 2, par)

    def tensor_cycle(self, pe, i, par, exists):
        prev2, prev, cur, nxt, nxt2 = exists
        for c in range(HC):
            if cur:
                self.up_chunk(pe, i, par, c)
            if prev:
                self.down_chunk(pe, i - 1, 1 - par, c)
            if c == 2 and nxt:
                self.transpose_x(pe, i + 1)


def all_phases(nc, w, x_tiles, tok_w, tok_b, w_all, proj_t, w1_t, b1, w2, txt, patches, mixed, out):
    with ExitStack() as ctx:
        def sb(name, shape, dt=F32):
            return ctx.enter_context(nc.sbuf_tensor(name, shape, dt))

        def ps(name, shape):
            return ctx.enter_context(nc.psum_tensor(name, shape, F32))

        def sem(name):
            return ctx.enter_context(nc.semaphore(name))

        eps_tile = sb("eps_tile", [P, 1])
        pow_tile = sb("pow_tile", [SEQ, G])
        ln_eps = sb("ln_eps", [SEQ, G])

        h_in = sb("h_in", [SEQ, G, DIM])
        bn_st = sb("bn_st", [SEQ, G, 6])
        bn_mv = sb("bn_mv", [SEQ, G, 2])
        var_eps = sb("var_eps", [SEQ, G])
        rstd = sb("rstd", [SEQ, G])
        carrier = sb("carrier", [1, 1])
        xn = sb("xn", [SEQ, G, DIM])
        xt0 = sb("xt0", [P, 2, GT], F32R)
        xt1 = sb("xt1", [P, GT], F32R)
        qk_hi = sb("qk_hi", [HALF, 4, GT], F32R)
        qk_lo = sb("qk_lo", [HALF, 4, GT], F32R)
        qk_sq = [sb(f"qk_sq{s}", [HALF, 4, GT]) for s in range(2)]
        stack = [sb(f"stack{s}", [P, 3, 4, GT], F32R) for s in range(2)]
        v_all = [sb(f"v_aug{s}", [P, G, HEADS, VW]) for s in range(2)]
        v_aug = [v[0:SEQ] for v in v_all]
        bounds = sb("bounds", [SEQ, G, P])
        stab_k = sb("stab_k", [P, G])
        bound_k = sb("bound_k", [FEAT, G, SEQ])
        nb_q = sb("nb_q", [P, GT], F32R)
        nb_k = sb("nb_k", [P, GT], F32R)
        qp = sb("qp", [P, PAIRS, GT])
        kp_all = sb("kp", [P, G, HEADS * FEAT])
        kp = kp_all[0:SEQ]
        context = sb("context", [P, G, PAIRS, 2 * VW])
        den = sb("den", [SEQ, G, HEADS])
        attn = sb("attn", [SEQ, G, DIM])
        ot0 = sb("ot0", [P, 2, GT], F32R)
        ot1 = sb("ot1", [P, GT], F32R)
        h_res = sb("h_res", [SEQ, G, DIM])
        h_out = sb("h_out", [SEQ, G, DIM])

        tr = [ps("tr0", [P, 512]), ps("tr1", [P, 512])]
        pj_banks = ps("pj", [P, 2, 512])
        pj = [pj_banks[:, 0], pj_banks[:, 1]]
        wide = ps("wide", [P, 4, 512])

        w0_raw, w1_raw, w1a_raw, w1b_raw = (kp_all[:, b] for b in range(G))
        w2_raw = qp[:].rearrange("p q t -> p (q t)")[:, 0:HC * DIM].rearrange("p (c n) -> p c n", c=HC)
        raw = [sb(f"emb_raw{n}", [P, KC, SUB * P])[:] for n in range(LOADS)]
        proj_raw = sb("proj_raw", [QUAD, P])
        proj_sc = sb("proj_sc", [QUAD, P])
        sel_raw = sb("sel_raw", [QUAD, HEADS // 2 * FEAT])
        e = Embedding(nc, ctx, raw, [wide[:, s] for s in range(RING)], x_tiles, tok_w, tok_b, patches)

        const_pool = sem("const_pool")
        proj_cleared = sem("proj_cleared")
        stack_cleared = sem("stack_cleared")
        kp_cleared = sem("kp_cleared")
        const_ready = sem("const_ready")
        att_raw_in = sem("att_raw_in")
        ffn_raw_in = sem("ffn_raw_in")
        ffn_late_in = sem("ffn_late_in")
        att_weights = sem("att_weights")
        ffn_weights = sem("ffn_weights")
        h_loaded = sem("h_loaded")
        stats = sem("stats")
        moments = sem("moments")
        var_ready = sem("var_ready")
        rstd_ready = sem("rstd_ready")
        xn_ready = sem("xn_ready")
        x_transposed = sem("x_transposed")
        xt_hi = sem("xt_hi")
        xt_lo = sem("xt_lo")
        qk_mm = sem("qk_mm")
        qk_hi_ready = sem("qk_hi_ready")
        qk_sq_ready = sem("qk_sq_ready")
        qk_lo_ready = sem("qk_lo_ready")
        stacked = sem("stacked")
        v_mm = sem("v_mm")
        v_ready = sem("v_ready")
        dash_mm = sem("dash_mm")
        maxed = sem("maxed")
        diag_mm = sem("diag_mm")
        bounds_tr = sem("bounds_tr")
        stab_ready = sem("stab_ready")
        bound_k_ready = sem("bound_k_ready")
        nbk_hi = sem("nbk_hi")
        nbk_ready = sem("nbk_ready")
        nbq_hi = sem("nbq_hi")
        nbq_ready = sem("nbq_ready")
        fq_mm = sem("fq_mm")
        fk_mm = sem("fk_mm")
        qp_exp = sem("qp_exp")
        kp_exp = sem("kp_exp")
        qp_ready = sem("qp_ready")
        kp01_ready = sem("kp01_ready")
        kp23_ready = sem("kp23_ready")
        ctx_mm = sem("ctx_mm")
        ctx_ready = sem("ctx_ready")
        att_mm = sem("att_mm")
        den_ready = sem("den_ready")
        attn_ready = sem("attn_ready")
        o_transposed = sem("o_transposed")
        ot_hi = sem("ot_hi")
        ot_lo = sem("ot_lo")
        wo_mm = sem("wo_mm")
        res_loaded = sem("res_loaded")
        res_ready = sem("res_ready")
        h_stored = sem("h_stored")
        f = FeedForward(nc, ctx, w, e, (pj, [wide[:, 0], wide[:, 1]], [tr, [wide[:, 2], wide[:, 3]]]),
                        mixed, h_stored, out)
        block = ctx.enter_context(nc.Block())

        def tok(b):
            return slice(b * SEQ, (b + 1) * SEQ)

        def passes(c0, c1, x0, x1, t):
            return split_passes(w.w0_hi[:, c0:c1], w.w0_lo[:, c0:c1], w.w1_hi[:, c0:c1], w.w1_lo[0:REST, c0:c1],
                                x0[:, 0, t], x0[:, 1, t], x1[:, t])

        OUTPUT_BANKS = (2, 3, 0, 1)
        LAST_OUTPUT_BANKS = (2, 3, 2, 3)

        def feature_banks(b):
            return (wide[0:SEQ, 2:4], wide[0:SEQ, 0:2], pj_banks[0:SEQ], wide[0:SEQ, 2:4])[b][:, :, 0:3 * P]

        WARM_UP = 3
        LOOP_FROM, LOOP_TO = 3, GROUPS - 3

        def pipeline(eng, emit):
            def single(i):
                emit(i, i % 2, [0 <= i + d < GROUPS for d in (-2, -1, 0, 1, 2)])

            for i in range(LOOP_FROM):
                single(i)
            with eng.Fori(LOOP_FROM, LOOP_TO - 1, 2) as i:
                emit(i, LOOP_FROM % 2, [True] * 5)
                emit(i + 1, (LOOP_FROM + 1) % 2, [True] * 5)
            for i in range(LOOP_TO, GROUPS):
                single(i)

        patch_rows = patches.rearrange("(b n) d -> b n d", n=PATCHES)

        @block.sync
        def _(sp):
            def load_tokens(g, dst, done):
                sp.dma_start(dst[0:PATCHES], patch_rows[bass.ds(g * G, G)].rearrange("b s d -> s b d")
                             ).then_inc(done, 16)
                sp.dma_start(dst[PATCHES:SEQ], txt[bass.ds(g * G, G)].rearrange("b s d -> s b d")
                             ).then_inc(done, 16)

            def load(g):
                sp.wait_ge(xn_ready, since(G * g))
                load_tokens(g, h_in, h_loaded)

            def load_residual(g):
                sp.wait_ge(res_ready, since(G * g))
                load_tokens(g, h_res, res_loaded)

            def store(g):
                sp.wait_ge(res_ready, G * (g + 1))
                sp.dma_start(mixed[bass.ds(g * G, G)].rearrange("b s d -> s b d"), h_out[:]).then_inc(h_stored, 16)

            def stack_up(g, par):
                sp.wait_ge(fq_mm, since(PAIRS * (g - 1)))
                sp.wait_ge(qk_hi_ready, 4 * (g + 1))
                for j in range(3):
                    for row in (0, 2):
                        sp.dma_start(stack[par][row * QUAD:(row + 1) * QUAD, j].bitcast(F32),
                                     qk_hi[j * QUAD:(j + 1) * QUAD].bitcast(F32)).then_inc(stacked, 16)
                sp.wait_ge(qk_lo_ready, 4 * (g + 1))
                for j in range(3):
                    sp.dma_start(stack[par][QUAD:2 * QUAD, j].bitcast(F32),
                                 qk_lo[j * QUAD:(j + 1) * QUAD].bitcast(F32)).then_inc(stacked, 16)

            e.sync_first(sp)
            sp.dma_start(w0_raw, w_all[0:P, :]).then_inc(att_raw_in, 16)
            sp.dma_start(w1_raw[0:REST], w_all[P:DIM, :]).then_inc(att_raw_in, 16)
            sp.dma_start(w1_raw[REST:P], w_all[P:DIM, :]).then_inc(att_raw_in, 16)
            sp.wait_ge(proj_cleared, 1)
            for r in range(2):
                sp.dma_start(proj_raw[r * DH:(r + 1) * DH, r * FEAT:(r + 1) * FEAT], proj_t).then_inc(att_raw_in, 16)

            def first_group():
                for s in range(2):
                    sp.wait_ge(e.stored[s], 16)
                load(0)

            def tile_and_weights(sp, r, u):
                e.sync_tile(sp, r, u)
                if isinstance(r, int) and r == 0 and u == 3:
                    sp.dma_start(w1a_raw, w1_t[0:P, :]).then_inc(ffn_raw_in, 16)
                if isinstance(r, int) and r == 0 and u == 5:
                    sp.dma_start(w1b_raw[0:REST], w1_t[P:DIM, :]).then_inc(ffn_raw_in, 16)
                    sp.dma_start(w1b_raw[REST:P], w1_t[P:DIM, :]).then_inc(ffn_raw_in, 16)

            e.rounds(sp, tile_and_weights, first_group)
            sp.dma_start(w.b1[:], b1).then_inc(ffn_late_in, 16)
            sp.dma_start(w2_raw, w2.rearrange("(c p) n -> p c n", p=P)).then_inc(ffn_late_in, 16)
            for u in range(BODY):
                e.sync_tile(sp, ROUNDS - 1, u, False)
                if u == 1:
                    load(1)
                if u == 3:
                    stack_up(0, 0)
            for s in range(RING):
                sp.wait_ge(e.stored[s], 16 * EMB_TILES // RING)
            load_residual(0)

            def emit(i, par, exists):
                prev2, prev, cur, nxt, nxt2 = exists
                if nxt2:
                    load(i + 2)
                elif nxt:
                    f.load(sp, 0, 0)
                if prev2:
                    store(i - 2)
                    load_residual(i - 1)
                if nxt:
                    stack_up(i + 1, 1 - par)

            pipeline(sp, emit)
            f.load(sp, 1, 1)
            f.load_residual(sp, 0)
            store(GROUPS - 2)
            load_residual(GROUPS - 1)
            f.load(sp, 2, 0)
            f.load(sp, 3, 1)
            store(GROUPS - 1)
            sp.wait_ge(h_stored, 16 * GROUPS)
            f.pipeline(sp, f.sync_cycle)
            sp.wait_ge(f.stored, 16 * F_ITERS)

        @block.gpsimd
        def _(pool):
            for s in range(2):
                nc.gpsimd.memset(v_all[s][:], 1.0).then_inc(const_pool, 1)
            nc.gpsimd.memset(pow_tile[:], -0.5).then_inc(const_pool, 1)
            nc.gpsimd.memset(f.pow_tile[:], -0.5).then_inc(const_pool, 1)
            nc.gpsimd.memset(f.ln_eps[:], LN_EPS).then_inc(const_pool, 1)
            nc.gpsimd.memset(ln_eps[:], LN_EPS).then_inc(const_pool, 1)
            nc.gpsimd.memset(eps_tile[:], KERNEL_EPS).then_inc(const_pool, 1)
            nc.gpsimd.memset(bounds[:], 0.0).then_inc(const_pool, 1)
            nc.gpsimd.memset(context[:], 0.0).then_inc(const_pool, 1)
            nc.gpsimd.memset(proj_raw[:], 0.0).then_inc(proj_cleared, 1)
            steps = {}

            def chained(done, ins):
                steps[done] = steps.get(done, 0) + 1
                ins.then_inc(done, 1)
                pool.wait_ge(done, steps[done])

            chained(const_ready, nc.gpsimd.memset(w.ident[:], 1.0))
            chained(const_ready, nc.gpsimd.memset(sel_raw[:], -1.0))
            chained(const_ready, nc.gpsimd.memset(w.sel[:].bitcast(F32), 0.0))
            chained(const_ready, nc.gpsimd.memset(w.diag_w[:], 0.5 * DH ** -0.5))
            chained(const_ready, nc.gpsimd.affine_select(out=w.ident[:], in_=w.ident[:], compare_op=ALU.is_equal, fill=0.0,
                                                         base=0, pattern=[[-1, P]], channel_multiplier=1))
            chained(const_ready, nc.gpsimd.affine_select(out=sel_raw[:], in_=sel_raw[:], compare_op=ALU.is_ge, fill=0.0,
                                                         base=0, pattern=[[1, HEADS // 2 * FEAT]],
                                                         channel_multiplier=-FEAT))
            chained(const_ready, nc.gpsimd.affine_select(out=w.diag_w[:], in_=w.diag_w[:], compare_op=ALU.is_ge, fill=0.0,
                                                         base=0, pattern=[[-DH, QUAD]], channel_multiplier=1))
            chained(const_ready, nc.gpsimd.affine_select(out=sel_raw[:], in_=sel_raw[:], compare_op=ALU.is_ge, fill=0.0,
                                                         base=FEAT - 1, pattern=[[-1, HEADS // 2 * FEAT]],
                                                         channel_multiplier=FEAT))
            chained(const_ready, nc.gpsimd.affine_select(out=w.diag_w[:], in_=w.diag_w[:], compare_op=ALU.is_ge, fill=0.0,
                                                         base=DH - 1, pattern=[[DH, QUAD]], channel_multiplier=-1))
            for n in range(P // QUAD):
                half = (n % 2) * (HEADS // 2) * FEAT
                chained(const_ready, nc.gpsimd.tensor_copy(w.sel[n * QUAD:(n + 1) * QUAD, half:half + HEADS // 2 * FEAT],
                                                           sel_raw[:]))

            pool.wait_ge(att_raw_in, 16 * 5)
            splits = ((w0_raw, w.w0_hi[:], w.w0_lo[:]), (w1_raw, w.w1_hi[:], w.w1_lo[:]))
            for value, hi, lo in splits:
                chained(att_weights, nc.gpsimd.tensor_copy(hi, value))
                chained(att_weights, nc.gpsimd.tensor_tensor(lo, value, hi.bitcast(F32), ALU.subtract))
            chained(att_weights, nc.gpsimd.tensor_scalar(proj_sc[:], proj_raw[:], DH ** -0.25, None, ALU.mult))
            chained(att_weights, nc.gpsimd.tensor_copy(w.proj_st[0:QUAD], proj_sc[:]))
            chained(att_weights, nc.gpsimd.tensor_copy(w.proj_st[QUAD:2 * QUAD], proj_sc[:]))
            chained(att_weights, nc.gpsimd.tensor_tensor(w.proj_st[2 * QUAD:3 * QUAD], proj_sc[:],
                                                         w.proj_st[0:QUAD].bitcast(F32), ALU.subtract))
            chained(att_weights, nc.gpsimd.memset(w.proj_st[3 * QUAD:P].bitcast(F32), 0.0))

            def root(g):
                pool.wait_ge(moments, G * (g + 1))
                pool.wait_ge(xn_ready, since(G * g))
                nc.gpsimd.tensor_tensor(var_eps[:], bn_mv[:, :, 1], ln_eps[:], ALU.add).then_inc(var_ready, 1)
                pool.wait_ge(var_ready, g + 1)
                nc.gpsimd.tensor_tensor(rstd[:], var_eps[:], pow_tile[:], ALU.pow).then_inc(rstd_ready, 1)

            pool.wait_ge(const_pool, 9)

            def split(value, hi, lo):
                chained(ffn_weights, nc.gpsimd.tensor_copy(hi, value))
                chained(ffn_weights, nc.gpsimd.tensor_tensor(lo, value, hi.bitcast(F32), ALU.subtract))

            pool.wait_ge(ffn_raw_in, 16 * 3)
            split(w1a_raw, w.w1a_hi[:], w.w1a_lo[:])
            root(0)
            split(w1b_raw, w.w1b_hi[:], w.w1b_lo[:])
            chained(kp_cleared, nc.gpsimd.memset(kp_all[P // 2:P], 0.0))
            pool.wait_ge(ffn_late_in, 16 * 2)
            split(w2_raw, w.w2_parts[:, :, 0], w.w2_parts[:, :, 1])
            root(1)

            def emit(i, par, exists):
                prev2, prev, cur, nxt, nxt2 = exists
                if nxt2:
                    root(i + 2)
                elif not nxt:
                    f.root(pool, 0, 0)
                if cur:
                    for b in (2, 3):
                        pool.wait_ge(kp_exp, G * i + b + 1)
                        nc.gpsimd.tensor_tensor(kp[:, b], kp[:, b],
                                                eps_tile[0:SEQ].to_broadcast([SEQ, HEADS * FEAT]),
                                                ALU.add).then_inc(kp23_ready, 1)
                    for p in range(PAIRS):
                        pool.wait_ge(qp_exp, PAIRS * i + p + 1)
                        nc.gpsimd.tensor_tensor(qp[:, p], qp[:, p], eps_tile[:].to_broadcast([P, GT]),
                                                ALU.add).then_inc(qp_ready, 1)

            pipeline(pool, emit)
            for g in (1, 2, 3):
                f.root(pool, g, g % 2)
            f.pipeline(pool, f.gpsimd_cycle)

        @block.scalar
        def _(act):
            def transposed_hi(g):
                act.wait_ge(v_mm, since(G * g))
                act.wait_ge(x_transposed, 2 * g + 1)
                nc.scalar.activation(xt0[:, 0], pj[1][:, 0:GT], ACT.Copy).then_inc(xt_hi, 1)
                act.wait_ge(x_transposed, 2 * g + 2)
                nc.scalar.activation(xt1[0:REST], pj[0][0:REST, 0:GT], ACT.Copy).then_inc(xt_hi, 1)

            def qk_parts(g, par, chunks):
                if chunks[0] == 0:
                    act.wait_ge(stacked, since(16 * 9 * g))
                    act.wait_ge(diag_mm, since(g - 1))
                for c in chunks:
                    act.wait_ge(qk_mm, 4 * g + c + 1)
                    nc.scalar.activation(qk_hi[:, c], pj[c % 2][0:HALF, 0:GT],
                                         ACT.Copy).then_inc(qk_hi_ready, 1)
                    nc.scalar.activation(qk_sq[par][:, c], pj[c % 2][0:HALF, 0:GT],
                                         ACT.Square).then_inc(qk_sq_ready, 1)

            def exp_k(g):
                act.wait_ge(ctx_mm, since(G * g))
                for b in range(G):
                    act.wait_ge(fk_mm, G * g + b + 1)
                    nc.scalar.activation(kp[:, b].rearrange("p (a c) -> p a c", a=2), feature_banks(b),
                                         ACT.Exp).then_inc(kp_exp, 1)

            def exp_q(g, pairs):
                act.wait_ge(att_mm, since(G * g))
                for p in pairs:
                    act.wait_ge(fq_mm, PAIRS * g + p + 1)
                    nc.scalar.activation(qp[:, p], wide[:, p % 4, 0:GT], ACT.Exp).then_inc(qp_exp, 1)

            def copy_context(g, n):
                if n == 0:
                    act.wait_ge(att_mm, since(G * g))
                act.wait_ge(ctx_mm, G * g + 2 * n + 2)
                for r in range(2):
                    rows, cols = slice(r * FEAT, (r + 1) * FEAT), slice(r * VW, (r + 1) * VW)
                    nc.scalar.activation(
                        context[rows, 2 * n:2 * n + 2, :, cols],
                        tr[n][rows, 0:2 * PAIRS * 2 * VW].rearrange(
                            "p (b q c) -> p b q c", b=2, q=PAIRS)[:, :, :, cols],
                        ACT.Copy).then_inc(ctx_ready, 1)

            def copy_values(g, par, b):
                act.wait_ge(v_mm, G * g + b + 1)
                if b == 0:
                    act.wait_ge(ctx_mm, since(G * (g - 1)))
                nc.scalar.activation(v_aug[par][:, b, :, 0:DH],
                                     pj[b % 2][0:SEQ, 0:DIM].rearrange("p (h d) -> p h d", h=HEADS),
                                     ACT.Copy).then_inc(v_ready, 1)

            def output_hi(g):
                act.wait_ge(wo_mm, since(G * g))
                act.wait_ge(o_transposed, 2 * g + 1)
                nc.scalar.activation(ot0[:, 0], pj[1][:, 0:GT], ACT.Copy).then_inc(ot_hi, 1)
                act.wait_ge(o_transposed, 2 * g + 2)
                nc.scalar.activation(ot1[0:REST], pj[0][0:REST, 0:GT], ACT.Copy).then_inc(ot_hi, 1)

            e.rounds(act, e.scalar_tile)
            for u in range(BODY):
                e.scalar_tile(act, ROUNDS - 1, u)
                if u == 2:
                    transposed_hi(0)
                if u == 4:
                    qk_parts(0, 0, (0, 1))
            qk_parts(0, 0, (2, 3))
            act.wait_ge(const_pool, 9)
            act.wait_ge(ffn_weights, 6)
            act.wait_ge(kp_cleared, 1)

            def emit(i, par, exists):
                prev2, prev, cur, nxt, nxt2 = exists
                if prev:
                    copy_context(i - 1, 0)
                if cur:
                    for b in range(G):
                        copy_values(i, par, b)
                if nxt:
                    transposed_hi(i + 1)
                elif cur:
                    f.transposed_hi(act, 0, 0)
                if prev:
                    copy_context(i - 1, 1)
                if nxt:
                    qk_parts(i + 1, 1 - par, range(4))
                if cur:
                    exp_k(i)
                    exp_q(i, (0, 1))
                if prev:
                    output_hi(i - 1)
                if cur:
                    exp_q(i, (2, 3, 4, 5))

            pipeline(act, emit)
            g = GROUPS - 1
            f.gelu(act, 0, 0, False)
            copy_context(g, 0)
            f.gelu(act, 0, 1, False)
            f.gelu(act, 0, 2, False)
            copy_context(g, 1)
            f.gelu(act, 0, 3, False)
            f.transposed_hi(act, 1, 1)
            f.gelu(act, 0, 4, False)
            f.gelu(act, 0, 5, False)
            output_hi(g)
            for c in range(HC):
                f.gelu(act, 1, c, True)
                if c == 3:
                    f.transposed_hi(act, 2, 0)
            f.pipeline(act, f.scalar_cycle)

        @block.vector
        def _(dve):
            def take_moments(g):
                dve.wait_ge(h_loaded, 32 * (g + 1))
                for b in range(G):
                    nc.vector.bn_stats(bn_st[:, b], h_in[:, b]).then_inc(stats, 1)
                dve.wait_ge(stats, G * (g + 1))
                nc.vector.memset(carrier[:], 0.0)
                for b in range(G):
                    nc.vector.bn_aggr(bn_mv[:, b], bn_st[:, b]).then_inc(moments, 1)

            def norm(g):
                dve.wait_ge(rstd_ready, g + 1)
                dve.wait_ge(x_transposed, since(2 * g))
                for b in range(G):
                    nc.vector.tensor_scalar(xn[:, b], h_in[:, b], bn_mv[:, b, 0:1], rstd[:, b:b + 1],
                                            ALU.subtract, ALU.mult).then_inc(xn_ready, 1)

            def transposed_lo(g):
                dve.wait_ge(xt_hi, 2 * g + 1)
                nc.vector.tensor_tensor(xt0[:, 1], pj[1][:, 0:GT], xt0[:, 0].bitcast(F32),
                                        ALU.subtract).then_inc(xt_lo, 1)
                dve.wait_ge(xt_hi, 2 * g + 2)
                nc.vector.tensor_tensor(xt1[REST:P], pj[0][0:REST, 0:GT], xt1[0:REST].bitcast(F32),
                                        ALU.subtract).then_inc(xt_lo, 1)

            def qk_rests(g, chunks):
                for c in chunks:
                    dve.wait_ge(qk_sq_ready, 4 * g + c + 1)
                    nc.vector.tensor_tensor(qk_lo[:, c], pj[c % 2][0:HALF, 0:GT],
                                            qk_hi[:, c].bitcast(F32), ALU.subtract).then_inc(qk_lo_ready, 1)

            def maxima(g, b):
                if b == 0:
                    dve.wait_ge(bounds_tr, since(g))
                for t in range(2):
                    dve.wait_ge(dash_mm, 8 * g + 2 * b + t + 1)
                    nc.vector.tensor_reduce(
                        bounds[:, b, 2 * t * QUAD:2 * (t + 1) * QUAD].rearrange(
                            "p (a h) -> p a h", a=2)[:, :, 0:HEADS // 2],
                        wide[0:SEQ, 2 * t:2 * t + 2, 0:3 * P].rearrange("p a (h m) -> p a h m", m=FEAT),
                        AX_X, ALU.max).then_inc(maxed, 1)

            def bound_of_k(g):
                dve.wait_ge(bounds_tr, g + 1)
                dve.wait_ge(bound_k_ready, since(g))
                nc.vector.tensor_reduce(stab_k[2 * QUAD:P],
                                        wide[2 * QUAD:P, 1, 0:GT].rearrange("p (b s) -> p b s", b=G),
                                        AX_X, ALU.max).then_inc(stab_ready, 1)
                dve.wait_ge(stab_ready, g + 1)
                dve.wait_ge(nbk_ready, since(g))
                nc.vector.tensor_tensor(bound_k[:],
                                        wide[2 * QUAD:P, 0, 0:GT].rearrange("p (b s) -> p b s", b=G),
                                        stab_k[2 * QUAD:P].unsqueeze(2).to_broadcast([FEAT, G, SEQ]),
                                        ALU.add).then_inc(bound_k_ready, 1)
                flat = bound_k[:].rearrange("p b s -> p (b s)")
                dve.wait_ge(bound_k_ready, g + 1)
                dve.wait_ge(fk_mm, since(G * g))
                nc.vector.tensor_copy(nb_k[0:FEAT], flat).then_inc(nbk_hi, 1)
                dve.wait_ge(nbk_hi, g + 1)
                nc.vector.tensor_tensor(nb_k[FEAT:P], flat, nb_k[0:FEAT].bitcast(F32),
                                        ALU.subtract).then_inc(nbk_ready, 1)

            def bound_of_q(g):
                dve.wait_ge(fq_mm, since(PAIRS * g))
                nc.vector.tensor_copy(nb_q[0:FEAT], wide[0:FEAT, 0, 0:GT]).then_inc(nbq_hi, 1)
                dve.wait_ge(nbq_hi, g + 1)
                nc.vector.tensor_tensor(nb_q[FEAT:P], wide[0:FEAT, 0, 0:GT], nb_q[0:FEAT].bitcast(F32),
                                        ALU.subtract).then_inc(nbq_ready, 1)

            def add_eps(g):
                for b in range(2):
                    dve.wait_ge(kp_exp, G * g + b + 1)
                    nc.vector.tensor_scalar(kp[:, b], kp[:, b], KERNEL_EPS, None, ALU.add).then_inc(kp01_ready, 1)

            def divide(g):
                dve.wait_ge(att_mm, G * (g + 1))
                dve.wait_ge(attn_ready, since(G * g))
                sums = [tr[n][0:SEQ, 0:2 * HEADS * VW].rearrange("p (b h c) -> p b h c", b=2, h=HEADS)
                        for n in range(2)]
                for n in range(2):
                    nc.vector.reciprocal(den[:, 2 * n:2 * n + 2], sums[n][:, :, :, DH]).then_inc(den_ready, 1)
                dve.wait_ge(o_transposed, since(2 * g))
                for n in range(G):
                    dve.wait_ge(den_ready, 2 * g + 1 + n // 2)
                    nc.vector.tensor_tensor(attn[:, n].rearrange("p (h d) -> p h d", h=HEADS),
                                            sums[n // 2][:, n % 2, :, 0:DH],
                                            den[:, n].unsqueeze(2).to_broadcast([SEQ, HEADS, DH]),
                                            ALU.mult).then_inc(attn_ready, 1)

            def output_lo(g):
                dve.wait_ge(wo_mm, since(G * g))
                dve.wait_ge(ot_hi, 2 * g + 1)
                nc.vector.tensor_tensor(ot0[:, 1], pj[1][:, 0:GT], ot0[:, 0].bitcast(F32),
                                        ALU.subtract).then_inc(ot_lo, 1)
                dve.wait_ge(ot_hi, 2 * g + 2)
                nc.vector.tensor_tensor(ot1[REST:P], pj[0][0:REST, 0:GT], ot1[0:REST].bitcast(F32),
                                        ALU.subtract).then_inc(ot_lo, 1)

            def residual(g, banks):
                dve.wait_ge(res_loaded, 32 * (g + 1))
                dve.wait_ge(h_stored, since(16 * g))
                for b in range(G):
                    dve.wait_ge(wo_mm, G * g + b + 1)
                    nc.vector.tensor_tensor(h_out[:, b], wide[0:SEQ, banks[b], 0:DIM], h_res[:, b],
                                            ALU.add).then_inc(res_ready, 1)

            nc.vector.memset(stack[0][3 * QUAD:P].bitcast(F32), 0.0).then_inc(stack_cleared, 1)
            e.vector_first(dve)
            e.rounds(dve, e.vector_tile)
            for u in range(BODY):
                e.vector_tile(dve, ROUNDS - 1, u)
                if u == 0:
                    take_moments(0)
                if u == 1:
                    norm(0)
                if u == 2:
                    transposed_lo(0)
                if u == 4:
                    qk_rests(0, (0, 1))
            qk_rests(0, (2, 3))
            for u in (BODY - 2, BODY - 1):
                e.vector_finish(dve, ROUNDS - 1, u)
            take_moments(1)
            nc.vector.memset(stack[1][3 * QUAD:P].bitcast(F32), 0.0).then_inc(stack_cleared, 1)
            dve.wait_ge(const_pool, 9)

            def emit(i, par, exists):
                prev2, prev, cur, nxt, nxt2 = exists
                if nxt:
                    norm(i + 1)
                elif cur:
                    f.take_moments(dve, 0, 0)
                if prev2:
                    residual(i - 2, OUTPUT_BANKS)
                if cur:
                    maxima(i, 0)
                    maxima(i, 1)
                    maxima(i, 2)
                if nxt:
                    transposed_lo(i + 1)
                elif cur:
                    f.norm(dve, 0, 0)
                if cur:
                    maxima(i, 3)
                if nxt:
                    qk_rests(i + 1, (0, 1))
                elif cur:
                    f.transposed_lo(dve, 0, 0)
                if cur:
                    bound_of_k(i)
                    bound_of_q(i)
                if nxt:
                    qk_rests(i + 1, (2, 3))
                if prev:
                    divide(i - 1)
                if cur:
                    add_eps(i)
                if nxt2:
                    take_moments(i + 2)
                if prev:
                    output_lo(i - 1)
                if not nxt:
                    f.take_moments(dve, 1, 1)

            pipeline(dve, emit)
            g = GROUPS - 1
            f.hidden_lo(dve, 0, 0, False)
            residual(g - 1, LAST_OUTPUT_BANKS)
            f.norm(dve, 1, 1)
            for c in (1, 2, 3):
                f.hidden_lo(dve, 0, c, False)
            f.transposed_lo(dve, 1, 1)
            f.take_moments(dve, 2, 0)
            divide(g)
            f.hidden_lo(dve, 0, 4, False)
            f.hidden_lo(dve, 0, 5, False)
            output_lo(g)
            f.norm(dve, 2, 0)
            for c in range(HC):
                f.hidden_lo(dve, 1, c, True)
                if c == 1:
                    residual(g, LAST_OUTPUT_BANKS)
                if c == 3:
                    f.transposed_lo(dve, 2, 0)
                    f.take_moments(dve, 3, 1)
            f.pipeline(dve, f.vector_cycle)

        @block.tensor
        def _(pe):

            def transpose_x(g):
                pe.wait_ge(xn_ready, G * (g + 1))
                pe.wait_ge(v_ready, since(G * g))
                for cols, out in ((slice(0, P), pj[1]), (slice(P, DIM), pj[0][0:REST])):
                    for b in range(G):
                        last = nc.tensor.transpose(out[:, tok(b)], xn[:, b, cols], w.ident[0:SEQ, 0:SEQ])
                    last.then_inc(x_transposed, 1)

            def project_qk(g, chunks):
                for c in chunks:
                    if c == 0:
                        pe.wait_ge(xt_lo, 2 * (g + 1))
                    if c >= 2:
                        pe.wait_ge(qk_lo_ready, 4 * g + c - 1)
                    ps5 = passes(c * HALF, (c + 1) * HALF, xt0, xt1, slice(0, GT))
                    for n, (wt, x) in enumerate(ps5):
                        last = nc.tensor.matmul(pj[c % 2][0:HALF, 0:GT], wt, x, start=(n == 0), stop=(n == 4))
                    last.then_inc(qk_mm, 1)

            def values(g, b):
                if b < 2:
                    pe.wait_ge(qk_lo_ready, 4 * g + b + 3)
                else:
                    pe.wait_ge(v_ready, G * g + b - 1)
                ps5 = passes(2 * DIM, 3 * DIM, xt0, xt1, tok(b))
                for n, (wt, x) in enumerate(ps5):
                    last = nc.tensor.matmul(pj[b % 2][0:SEQ, 0:DIM], x, wt, start=(n == 0), stop=(n == 4))
                last.then_inc(v_mm, 1)

            def context_of(g, par, b, pairs=range(PAIRS)):
                if b < 2:
                    pe.wait_ge(kp01_ready, 2 * g + b + 1)
                    if b == 0:
                        pe.wait_ge(attn_ready, since(G * g))
                else:
                    pe.wait_ge(kp23_ready, 2 * g + b - 1)
                for p in pairs:
                    o = (b % 2) * PAIRS * 2 * VW + p * 2 * VW
                    last = nc.tensor.matmul(
                        tr[b // 2][:, o:o + 2 * VW], kp_all[:, b, p * P:(p + 1) * P],
                        v_all[par][:, b, 2 * p:2 * p + 2].rearrange("p h d -> p (h d)"), start=True, stop=True)
                if pairs[-1] == PAIRS - 1:
                    last.then_inc(ctx_mm, 1)

            def attend(g, b):
                if b == 0:
                    pe.wait_ge(qp_ready, PAIRS * (g + 1))
                if b % 2 == 0:
                    pe.wait_ge(ctx_ready, 4 * g + b + 2)
                for p in range(PAIRS):
                    o = (b % 2) * PAIRS * 2 * VW + p * 2 * VW
                    last = nc.tensor.matmul(tr[b // 2][0:SEQ, o:o + 2 * VW],
                                            qp[:, p, tok(b)], context[:, b, p], start=True, stop=True)
                last.then_inc(att_mm, 1)

            def transpose_o(g):
                pe.wait_ge(attn_ready, G * (g + 1))
                for cols, out in ((slice(0, P), pj[1]), (slice(P, DIM), pj[0][0:REST])):
                    for b in range(G):
                        last = nc.tensor.transpose(out[:, tok(b)], attn[:, b, cols], w.ident[0:SEQ, 0:SEQ])
                    last.then_inc(o_transposed, 1)

            def dash(g, par, b):
                for t in range(2):
                    if b:
                        pe.wait_ge(maxed, 8 * g + 2 * (b - 1) + t + 1)
                    for p in range(PAIRS):
                        c, j = 2 * t + p // 3, p % 3
                        last = nc.tensor.matmul(wide[0:SEQ, c, j * P:(j + 1) * P],
                                                stack[par][:, j, c, tok(b)], w.proj_st[:], start=True, stop=True)
                    last.then_inc(dash_mm, 1)

            def diag_of(g, par):
                pe.wait_ge(maxed, 8 * g + 7)
                for c in range(4):
                    last = nc.tensor.matmul(wide[c * QUAD:(c + 1) * QUAD, 0, 0:GT], w.diag_w[:], qk_sq[par][:, c],
                                            start=True, stop=(c >= 2), skip_group_check=True)
                last.then_inc(diag_mm, 1)

            def transpose_bounds(g):
                pe.wait_ge(maxed, 8 * g + 8)
                for b in range(G):
                    nc.tensor.matmul(wide[0:2 * QUAD, 0, tok(b)], bounds[:, b, 0:2 * QUAD], w.ident[0:SEQ, 0:SEQ],
                                     start=False, stop=True, skip_group_check=True)
                    last = nc.tensor.matmul(wide[2 * QUAD:P, 1, tok(b)], bounds[:, b, 2 * QUAD:P],
                                            w.ident[0:SEQ, 0:SEQ], start=True, stop=True)
                last.then_inc(bounds_tr, 1)

            def output(g, b, bank):
                if b == 0:
                    pe.wait_ge(ot_lo, 2 * (g + 1))
                ps5 = passes(3 * DIM, 4 * DIM, ot0, ot1, tok(b))
                for n, (wt, x) in enumerate(ps5):
                    last = nc.tensor.matmul(wide[0:SEQ, bank, 0:DIM], x, wt, start=(n == 0), stop=(n == 4))
                last.then_inc(wo_mm, 1)

            def features_k(g, par, nxt):
                for b in range(G):
                    if b == 0:
                        pe.wait_ge(nbk_ready, g + 1)
                    if b == 1:
                        pe.wait_ge(nbq_ready, g + 1)
                    if b == 2 and nxt:
                        pe.wait_ge(qk_lo_ready, 4 * (g + 2))
                    if b == 2 and not nxt:
                        pe.wait_ge(f.xt_lo, 2)
                    if b == 3:
                        pe.wait_ge(kp_exp, G * g + 1)
                    banks = feature_banks(b)
                    for a in range(2):
                        nc.tensor.matmul(banks[:, a], nb_k[:, tok(b)],
                                         w.sel[:, a * 3 * P:(a + 1) * 3 * P], start=True, stop=False,
                                         skip_group_check=True)
                        for j in range(3):
                            last = nc.tensor.matmul(banks[:, a, j * P:(j + 1) * P],
                                                    stack[par][:, j, 2 + a, tok(b)], w.proj_st[:],
                                                    start=False, stop=(j == 2), skip_group_check=True)
                    last.then_inc(fk_mm, 1)

            def features_q(g, par, pairs):
                for p in pairs:
                    if p in (0, 2):
                        pe.wait_ge(kp_exp, G * g + 2 + p)
                    if p >= 4:
                        pe.wait_ge(qp_exp, PAIRS * g + p - 3)
                    nc.tensor.matmul(wide[:, p % 4, 0:GT], w.proj_st[:], stack[par][:, p % 3, p // 3],
                                     start=True, stop=False)
                    nc.tensor.matmul(wide[:, p % 4, 0:GT], w.sel[:, p * P:(p + 1) * P], nb_q[:], start=False,
                                     stop=True).then_inc(fq_mm, 1)

            pe.wait_ge(const_pool, 1)
            ones = v_all[0][:].rearrange("p b h d -> p (b h d)")
            for _ in range(WARM_UP):
                nc.tensor.matmul(tr[0][:], ones[:, 0:P], ones[:, 0:512], start=True, stop=True)
            pe.wait_ge(e.w_split, 2)
            e.rounds(pe, e.tensor_tile)
            for u in range(BODY):
                e.tensor_tile(pe, ROUNDS - 1, u)
                if u == 1:
                    pe.wait_ge(const_ready, 13)
                    transpose_x(0)
                if u == 2:
                    pe.wait_ge(att_weights, 9)
                if 2 <= u <= 4:
                    project_qk(0, ((0, 1), (2,), (3,))[u - 2])
            pe.wait_ge(e.out_done, EMB_TILES)
            pe.wait_ge(const_pool, 9)
            pe.wait_ge(stack_cleared, 1)

            def emit(i, par, exists):
                prev2, prev, cur, nxt, nxt2 = exists
                if prev2:
                    for b in (0, 1):
                        pe.wait_ge(qp_exp, since(PAIRS * (i - 1) + b + 3))
                        output(i - 2, b, OUTPUT_BANKS[b])
                    context_of(i - 1, 1 - par, 1)
                    for b in (2, 3):
                        pe.wait_ge(qp_exp, since(PAIRS * (i - 1) + b + 3))
                        output(i - 2, b, OUTPUT_BANKS[b])
                if cur:
                    values(i, 0)
                    values(i, 1)
                if prev and not prev2:
                    pe.wait_ge(stack_cleared, 2)
                    context_of(i - 1, 1 - par, 1)
                if cur:
                    pe.wait_ge(stacked, 16 * 9 * (i + 1))
                    if prev2:
                        pe.wait_ge(res_ready, since(G * (i - 1)))
                    elif prev:
                        pe.wait_ge(qp_exp, since(PAIRS * i))
                    dash(i, par, 0)
                if prev:
                    context_of(i - 1, 1 - par, 2)
                if cur:
                    values(i, 2)
                    dash(i, par, 1)
                if prev:
                    context_of(i - 1, 1 - par, 3, (0, 1, 2))
                    attend(i - 1, 0)
                if cur:
                    values(i, 3)
                    dash(i, par, 2)
                if prev:
                    context_of(i - 1, 1 - par, 3, (3, 4, 5))
                if nxt:
                    transpose_x(i + 1)
                if prev:
                    attend(i - 1, 1)
                if cur:
                    dash(i, par, 3)
                if nxt:
                    project_qk(i + 1, (0, 1))
                elif cur:
                    pe.wait_ge(v_ready, G * GROUPS)
                    f.transpose_x(pe, 0)
                if cur:
                    diag_of(i, par)
                    transpose_bounds(i)
                if nxt:
                    project_qk(i + 1, (2, 3))
                if prev:
                    attend(i - 1, 2)
                    attend(i - 1, 3)
                if cur:
                    features_k(i, par, nxt)
                    features_q(i, par, (0, 1))
                if prev:
                    if cur:
                        pe.wait_ge(kp_exp, G * i + 3)
                    transpose_o(i - 1)
                if cur:
                    context_of(i, par, 0)
                    features_q(i, par, (2, 3, 4, 5))

            pipeline(pe, emit)
            g, par = GROUPS - 1, (GROUPS - 1) % 2
            context_of(g, par, 1)
            pe.wait_ge(ffn_weights, 6)
            pe.wait_ge(qp_exp, PAIRS * GROUPS)
            f.up_chunk(pe, 0, 0, 0)
            f.up_chunk(pe, 0, 0, 1)
            output(g - 1, 0, 2)
            output(g - 1, 1, 3)
            f.up_chunk(pe, 0, 0, 2)
            context_of(g, par, 2)
            for b in (2, 3):
                pe.wait_ge(res_ready, G * (g - 1) + b - 1)
                output(g - 1, b, b)
            f.up_chunk(pe, 0, 0, 3)
            context_of(g, par, 3)
            pe.wait_ge(ot_lo, 2 * g)
            f.transpose_x(pe, 1)
            for half in range(2):
                attend(g, 2 * half)
                attend(g, 2 * half + 1)
                f.up_chunk(pe, 0, 0, 4 + half)
            pe.wait_ge(f.xt_lo, 4)
            f.up_chunk(pe, 1, 1, 0)
            transpose_o(g)
            for c in range(HC):
                if c > 0:
                    f.up_chunk(pe, 1, 1, c)
                if c == 2:
                    for b in (2, 3):
                        pe.wait_ge(res_ready, G * g + b - 1)
                        output(g, b, b)
                f.down_chunk(pe, 0, 0, c)
                if c == 1:
                    for b in (0, 1):
                        pe.wait_ge(res_ready, G * (g - 1) + b + 3)
                        output(g, b, 2 + b)
                if c == 3:
                    f.transpose_x(pe, 2)
            f.pipeline(pe, f.tensor_cycle)


def build_program(nc, x_tiles, txt, tok_w, tok_b, w_all, proj_t, w1_t, b1, w2, out):
    patches = nc.dram_tensor("patches", (IMAGES * PATCHES, DIM), F32, kind="Internal").ap()
    mixed = nc.dram_tensor("mixed", (IMAGES, SEQ, DIM), F32, kind="Internal").ap()
    with ExitStack() as ctx:
        w = Weights(nc, ctx)
        all_phases(nc, w, x_tiles, tok_w, tok_b, w_all, proj_t, w1_t, b1, w2, txt, patches, mixed, out)


def kernel(**inputs):
    import concourse.bacc as bacc
    from concourse.bass_utils import run_bass_kernel_spmd

    a = {k: np.asarray(v) for k, v in inputs.items()}
    x = a["x"].reshape(IMAGES, GRID, PATCH, GRID, PATCH, CHANNELS).transpose(2, 4, 5, 0, 1, 3)
    x = x.reshape(KC, P, EMB_TILES // SUB, SUB * P).transpose(2, 1, 0, 3)
    layout = {
        "x_tiles": x,
        "txt_in": a["txt"],
        "tok_w": a["L0_tok_W"],
        "tok_b": a["L0_tok_b"],
        "w_all": np.concatenate([a["L0_attn_Wq"], a["L0_attn_Wk"], a["L0_attn_Wv"], a["L0_attn_Wo"]], axis=1),
        "proj_t": a["L0_attn_proj"].T,
        "w1_t": a["L0_ffn_in_weight"].T,
        "b1": a["L0_ffn_in_bias"].reshape(HC, P).T,
        "w2": a["L0_ffn_out_weight"],
    }
    nc = bacc.Bacc("TRN2", target_bir_lowering=False, num_devices=1)
    arrays, args = {}, []
    for name, value in layout.items():
        arrays[name] = np.ascontiguousarray(value)
        args.append(nc.dram_tensor(name, arrays[name].shape, F32, kind="ExternalInput").ap())
    out = nc.dram_tensor("out", (IMAGES, SEQ, DIM), F32, kind="ExternalOutput").ap()
    build_program(nc, *args, out)
    result = run_bass_kernel_spmd(nc, [arrays], core_ids=[0])
    return result.results[0]["out"]
```
